# Optimizing a Trainium2 kernel written in Bass

```python
import numpy as np
import jax
import jax.numpy as jnp

def _softmax(x, axis=-1):
    return jax.nn.softmax(x, axis=axis)

def _gelu(x):
    return jax.nn.gelu(x, approximate=True)

def _silu(x):
    return jax.nn.silu(x)

def _sigmoid(x):
    return jax.nn.sigmoid(x)

def _layernorm(x, axis=-1, eps=1e-05):
    m = jnp.mean(x, axis=axis, keepdims=True)
    v = jnp.var(x, axis=axis, keepdims=True)
    return (x - m) / jnp.sqrt(v + eps)

def _scatter_add(tgt, idx, src, axis=0):
    return tgt.at[idx].add(src)

def _segment_sum(src, seg, n):
    return jax.ops.segment_sum(src, seg, n)
kernel_name = 'mk_recurrent_d1_jaxref_r4_d471fe'

def setup_inputs(seed: int=0):
    np.random.seed(seed)
    _w = jnp.asarray

    def _L0_attn_setup():
        import jax, jax.numpy as jnp
        import numpy as np
        import math
        EMB = 256
        HEADS = 16
        B, S = (2, 512)
        key = jax.random.key(seed)
        k_x, k_wq, k_bq, k_wu, k_bu = jax.random.split(key, 5)
        lim = 1.0 / math.sqrt(EMB)
        x = jax.random.normal(k_x, (B, S, EMB), dtype=jnp.float32)
        wq = jax.random.uniform(k_wq, (EMB, EMB), jnp.float32, -lim, lim)
        bq = jax.random.uniform(k_bq, (EMB,), jnp.float32, -lim, lim)
        wu = jax.random.uniform(k_wu, (EMB, EMB), jnp.float32, -lim, lim)
        bu = jax.random.uniform(k_bu, (EMB,), jnp.float32, -lim, lim)
        return {'x': x, 'wq': wq, 'bq': bq, 'wu': wu, 'bu': bu}
    _L0_attn_in = _L0_attn_setup()

    def _L0_ffn_setup():
        import jax, jax.numpy as jnp
        import numpy as np
        B, S, H, F, G = (8, 512, 256, 1024, 128)
        EPS = 1e-05

        def _dequant(q, scales, g):
            K, N = q.shape
            w = (q.astype(jnp.float32) - 128.0).reshape(K // g, g, N) * scales[:, None, :]
            return w.reshape(K, N)
        key = jax.random.key(seed)
        ks = jax.random.split(key, 8)
        x = jax.random.normal(ks[0], (B, S, H), dtype=jnp.float32)
        ln_gamma = jnp.ones((H,), jnp.float32)
        ln_beta = jnp.zeros((H,), jnp.float32)
        fc1_q = jax.random.randint(ks[1], (H, F), 0, 64, dtype=jnp.int32)
        fc2_q = jax.random.randint(ks[2], (F, H), 0, 64, dtype=jnp.int32)
        fc1_scales = jax.random.uniform(ks[3], (H // G, F), jnp.float32) * 0.02 + 0.001
        fc2_scales = jax.random.uniform(ks[4], (F // G, H), jnp.float32) * 0.02 + 0.001
        fc1_bias = jax.random.normal(ks[5], (F,), jnp.float32) * 0.02
        fc2_bias = jax.random.normal(ks[6], (H,), jnp.float32) * 0.02
        return {'x': x, 'ln_gamma': ln_gamma, 'ln_beta': ln_beta, 'fc1_q': fc1_q, 'fc1_scales': fc1_scales, 'fc1_bias': fc1_bias, 'fc2_q': fc2_q, 'fc2_scales': fc2_scales, 'fc2_bias': fc2_bias}
    _L0_ffn_in = _L0_ffn_setup()
    _d = {'L0_attn_x': _L0_attn_in['x'], 'L0_attn_wq': _L0_attn_in['wq'], 'L0_attn_bq': _L0_attn_in['bq'], 'L0_attn_wu': _L0_attn_in['wu'], 'L0_attn_bu': _L0_attn_in['bu'], 'L0_ffn_ln_gamma': _L0_ffn_in['ln_gamma'], 'L0_ffn_ln_beta': _L0_ffn_in['ln_beta'], 'L0_ffn_fc1_q': _L0_ffn_in['fc1_q'], 'L0_ffn_fc1_scales': _L0_ffn_in['fc1_scales'], 'L0_ffn_fc1_bias': _L0_ffn_in['fc1_bias'], 'L0_ffn_fc2_q': _L0_ffn_in['fc2_q'], 'L0_ffn_fc2_scales': _L0_ffn_in['fc2_scales'], 'L0_ffn_fc2_bias': _L0_ffn_in['fc2_bias']}
    _x0 = _d['L0_attn_x']
    _d['L0_attn_x'] = jax.random.normal(jax.random.fold_in(jax.random.key(seed), 1), (2, 2048, 256), dtype=_x0.dtype)
    del _x0
    return _d

def reference(L0_attn_x, L0_attn_wq, L0_attn_bq, L0_attn_wu, L0_attn_bu, L0_ffn_ln_gamma, L0_ffn_ln_beta, L0_ffn_fc1_q, L0_ffn_fc1_scales, L0_ffn_fc1_bias, L0_ffn_fc2_q, L0_ffn_fc2_scales, L0_ffn_fc2_bias):

    def _L0_attn_ref(x, wq, bq, wu, bu):
        import jax, jax.numpy as jnp
        import numpy as np
        import math
        EMB = 256
        HEADS = 16
        B, S = (2, 512)
        b, s, emb = x.shape
        hd = emb // HEADS
        q = jnp.einsum('bse,oe->bso', x, wq) + bq
        qh = q.reshape(HEADS, b, s, hd)
        kh = qh
        vh = qh
        scale = 1.0 / math.sqrt(emb)
        scores = jnp.einsum('hbqd,hbkd->hbqk', qh, kh) * scale
        attn = jax.nn.softmax(scores, axis=-1)
        out = jnp.einsum('hbqk,hbkd->hbqd', attn, vh)
        out = out.reshape(b, s, emb)
        return jnp.einsum('bse,oe->bso', out, wu) + bu

    def _L0_ffn_ref(x, ln_gamma, ln_beta, fc1_q, fc1_scales, fc1_bias, fc2_q, fc2_scales, fc2_bias):
        import jax, jax.numpy as jnp
        import numpy as np
        B, S, H, F, G = (8, 512, 256, 1024, 128)
        EPS = 1e-05

        def _dequant(q, scales, g):
            K, N = q.shape
            w = (q.astype(jnp.float32) - 128.0).reshape(K // g, g, N) * scales[:, None, :]
            return w.reshape(K, N)
        residual = x
        mu = jnp.mean(x, axis=-1, keepdims=True)
        var = jnp.mean(jnp.square(x - mu), axis=-1, keepdims=True)
        h = (x - mu) * jax.lax.rsqrt(var + EPS) * ln_gamma + ln_beta
        hf = h.reshape(-1, H)
        w1 = _dequant(fc1_q, fc1_scales, G)
        y = hf @ w1 + fc1_bias
        y = jax.nn.silu(y)
        w2 = _dequant(fc2_q, fc2_scales, G)
        z = y @ w2 + fc2_bias
        return residual + 0.5 * z.reshape(residual.shape)
    x = L0_attn_x
    xn = _layernorm(x, axis=-1)
    s = _L0_attn_ref(xn, L0_attn_wq, L0_attn_bq, L0_attn_wu, L0_attn_bu)
    g = _silu(_L0_ffn_ref(xn, L0_ffn_ln_gamma, L0_ffn_ln_beta, L0_ffn_fc1_q, L0_ffn_fc1_scales, L0_ffn_fc1_bias, L0_ffn_fc2_q, L0_ffn_fc2_scales, L0_ffn_fc2_bias))
    x = x + s * g
    return x

_drawn_inputs = setup_inputs


def setup_inputs(seed=0):
    import zlib

    import numpy as np

    out = dict(_drawn_inputs(seed))
    spreads = {'L0_ffn_ln_gamma': (1.0, 0.2), 'L0_ffn_ln_beta': (0.0, 0.1)}
    factors = {'L0_attn_bq': 8.0,
     'L0_ffn_fc1_scales': 5.936,
     'L0_ffn_fc1_bias': 8.0,
     'L0_ffn_fc2_scales': 5.914,
     'L0_ffn_fc2_bias': 8.0}
    for name, (base, spread) in spreads.items():
        noise = np.random.default_rng([zlib.crc32(name.encode()), seed]).standard_normal(out[name].shape)
        drawn = base * np.exp(spread * noise) if base else spread * noise
        out[name] = jnp.asarray(drawn.astype(out[name].dtype))
    for name, factor in factors.items():
        out[name] = (out[name] * factor).astype(out[name].dtype)
    return out
```

```python
import concourse.bass as bass
from concourse import mybir
from contextlib import ExitStack

COMMON_MAX_LIMIT = 60.0


def attention_times_ffn_gate(
    nc: bass.Bass,
    x: bass.AP,
    wqT: bass.AP,
    bq: bass.AP,
    wuT: bass.AP,
    bu: bass.AP,
    ln_gamma: bass.AP,
    ln_beta: bass.AP,
    fc1_q: bass.AP,
    fc1_scales: bass.AP,
    fc1_bias: bass.AP,
    fc2_q: bass.AP,
    fc2_scales: bass.AP,
    fc2_bias: bass.AP,
    out: bass.AP,
    qT_scratch: bass.AP,
    shift_scratch: bass.AP,
):
    fp32 = mybir.dt.float32
    f32r = mybir.dt.float32r
    i32 = mybir.dt.int32
    ALU = mybir.AluOpType
    ACT = mybir.ActivationFunctionType
    AX = mybir.AxisListType

    P = 128
    ROWS, EMB = x.shape
    HD = 16
    CH = EMB // HD
    GROUPS = ROWS // P
    TOK = P * CH
    GPS = 4
    SETS = GROUPS // GPS
    SR = GPS * P
    EH = EMB // P
    F = fc1_q.shape[1]
    FC = F // P
    FB = EMB
    EPS = 1e-5
    SCALE = float(EMB) ** -0.5
    LN_STEPS = 16

    NB = 3
    QT = 512
    TILES = TOK // QT
    QUADS = CH // 4
    NQ = TILES * QUADS
    VW = 32
    STACK_DMAS = 6
    GEN_DMAS = 5

    x_set = x.rearrange("(s g r) e -> s r g e", g=GPS, r=P)
    x_grp = x.rearrange("(g r) e -> g r e", r=P)
    out_grp = out.rearrange("(g r) e -> g r e", r=P)
    qT_w = qT_scratch.rearrange("(s g) h p d (c r) -> s h p (d c) g r", g=GPS, r=P)
    qT_r = qT_scratch.rearrange("g h p d n -> g (p d) h n")
    sh_w = shift_scratch.rearrange("p (b k) r -> p k b r", k=P)
    sh_r = shift_scratch.rearrange("p (g c) r -> g p (c r)", c=CH)

    ctx = ExitStack()
    with ctx:
        def sb(name, shape, dt=fp32):
            return ctx.enter_context(nc.sbuf_tensor(name, shape, dt))

        def sem(name):
            return ctx.enter_context(nc.semaphore(name))

        q_rows = sb("q_rows", [P, GROUPS * EMB])
        gate = sb("gate", [P, GROUPS * EMB])
        ring = sb("ring", [P, NB * 4 * QT])
        keys = [sb(f"keys{b}", [P, TOK], f32r) for b in range(NB)]
        queries = [sb(f"queries{b}", [P, TOK], f32r) for b in range(NB)]
        values = [sb(f"values{b}", [P, CH, VW]) for b in range(NB)]
        w2 = sb("w2", [P, FC, EMB])
        wq_sb = sb("wq_sb", [P, EH, EMB])
        wu_sb = sb("wu_sb", [P, EH, EMB])
        bq_b = sb("bq_b", [P, EMB])
        bu_b = sb("bu_b", [P, EMB])
        b2_b = sb("b2_b", [P, EMB])
        b1_c = sb("b1_c", [P, FC])
        gamma_c = sb("gamma_c", [P, EH])
        beta_c = sb("beta_c", [P, EH])
        ident = sb("ident", [P, P])
        ones_row = sb("ones_row", [1, P])
        x_in = sb("x_in", [P, GPS, EMB])
        xn = sb("xn", [P, GPS, EMB])
        hn = sb("hn", [P, GPS, EMB])
        xnT = sb("xnT", [P, EH * SR])
        hT = sb("hT", [P, EH * SR])
        q_tile = sb("q_tile", [P, GPS, EMB])
        q_sq = sb("q_sq", [P, GPS * EMB])
        qT_hi = sb("qT_hi", [P, EH, GPS, P], f32r)
        qT_lo = sb("qT_lo", [P, EH, GPS, P], f32r)
        stats = sb("stats", [P, GPS, 6])
        mu = sb("mu", [P, GPS])
        ve = sb("ve", [P, GPS])
        sd = sb("sd", [P, GPS])
        rs = sb("rs", [P, GPS])
        nt = sb("nt", [P, GPS])
        norm2 = sb("norm2", [P, GROUPS * CH])
        shift = sb("shift", [P, GROUPS * CH])
        nmax = sb("nmax", [P, 1])
        top = sb("top", [1, 1])
        flag = sb("flag", [1, 1], i32)

        yT = ring[:, 0:FC * SR].rearrange("p (f n) -> p f n", f=FC)
        w1 = ring[:, FC * SR:FC * SR + EH * F].rearrange("p (k n) -> p k n", k=EH)
        st1 = q_rows[:, 0:EH * F].bitcast(i32)
        st1s = q_rows[:, EH * F:2 * EH * F]
        st2 = q_rows[:, 2 * EH * F:3 * EH * F].bitcast(i32)
        st2s = q_rows[:, 3 * EH * F:4 * EH * F]
        acc_sb = [xnT[:, 0:QT], xnT[:, QT:2 * QT]]
        x_re = [x_in[:, 0, :], x_in[:, 1, :]]
        attn = [x_in[:, 2, :], x_in[:, 3, :]]
        attnT = hT[:, 0:EH * P].rearrange("p (h n) -> p h n", h=EH)
        s_sb = [xn[:, 0, :], xn[:, 1, :]]
        res = [xn[:, 2, :], xn[:, 3, :]]
        sums = hn[:, 0, 0:4 * (HD + 1)].rearrange("p (c m) -> p c m", c=4)
        rden = hn[:, 1, 0:4]
        neg = hn[:, 2:4, :].rearrange("p a b -> p (a b)")
        neg_hi = qT_hi[:, 0, :, :].rearrange("p a b -> p (a b)")
        neg_lo = qT_lo[:, 0, :, :].rearrange("p a b -> p (a b)")

        PA, PB, PC, PD = [ctx.enter_context(nc.psum_tensor(f"pair{i}", [P, 2 * QT], fp32)) for i in range(4)]
        score_ps = [PA, PB, PC]
        acc_ps = [PD[:, 0:QT], PD[:, QT:2 * QT]]

        x_loaded = sem("x_loaded")
        small_loaded = sem("small_loaded")
        columns_loaded = sem("columns_loaded")
        w1_loaded = sem("w1_loaded")
        w2_loaded = sem("w2_loaded")
        wu_loaded = sem("wu_loaded")
        w1_ready = sem("w1_ready")
        w2_ready = sem("w2_ready")
        b2_halved = sem("b2_halved")
        consts_ready = sem("consts_ready")
        pool_step = sem("pool_step")
        ln_step = sem("ln_step")
        var_ready = sem("var_ready")
        sd_ready = sem("sd_ready")
        xn_ready = sem("xn_ready")
        hn_ready = sem("hn_ready")
        gate_seeded = sem("gate_seeded")
        xnT_in_psum = sem("xnT_in_psum")
        hT_in_psum = sem("hT_in_psum")
        xnT_ready = sem("xnT_ready")
        hT_ready = sem("hT_ready")
        q_in_psum = sem("q_in_psum")
        q_tile_ready = sem("q_tile_ready")
        q_rows_saved = sem("q_rows_saved")
        q_sq_ready = sem("q_sq_ready")
        norm2_ready = sem("norm2_ready")
        qT_in_psum = sem("qT_in_psum")
        qT_hi_ready = sem("qT_hi_ready")
        qT_lo_ready = sem("qT_lo_ready")
        qT_saved = sem("qT_saved")
        fc1_in_psum = sem("fc1_in_psum")
        y_ready = sem("y_ready")
        fc2_in_psum = sem("fc2_in_psum")
        z_added = sem("z_added")
        gate_ready = sem("gate_ready")
        shift_step = sem("shift_step")
        shift_pe = sem("shift_pe")
        flag_ready = sem("flag_ready")
        shift_ready = sem("shift_ready")
        neg_ready = sem("neg_ready")
        shift_saved = sem("shift_saved")
        gen_loaded = sem("gen_loaded")
        gen_scored = sem("gen_scored")
        gen_reduced = sem("gen_reduced")
        stack_loaded = [sem(f"stack_loaded{b}") for b in range(NB)]
        x_reloaded = [sem(f"x_reloaded{b}") for b in range(2)]
        values_ready = sem("values_ready")
        scored = sem("scored")
        exped = sem("exped")
        pv_done = sem("pv_done")
        acc_copied = sem("acc_copied")
        acc_turned = sem("acc_turned")
        acc_summed = sem("acc_summed")
        tail_step = sem("tail_step")
        attn_ready = sem("attn_ready")
        attnT_in_psum = sem("attnT_in_psum")
        attnT_ready = sem("attnT_ready")
        s_in_psum = sem("s_in_psum")
        s_ready = sem("s_ready")
        gated = sem("gated")
        res_ready = sem("res_ready")
        stored = [sem(f"stored{b}") for b in range(2)]

        def after(eng, s, count):
            if not isinstance(count, int) or count > 0:
                eng.wait_ge(s, count)

        def all_sets(eng, step):
            step(0)
            with eng.Fori(1, SETS - 1) as s:
                step(s)
            step(SETS - 1)

        def all_groups(eng, step):
            step(0, 0, True, False)
            with eng.Fori(0, (GROUPS - 2) // 6) as i:
                for u in range(6):
                    step(i * 6 + (u + 1), (u + 1) % 6, False, False)
            step(GROUPS - 1, (GROUPS - 1) % 6, False, True)

        block = ctx.enter_context(nc.Block())

        @block.sync
        def _(sp):
            def load_x(s):
                after(sp, xn_ready, s)
                sp.dma_start(x_in[:, :, :], x_set[s]).then_inc(x_loaded, 16)

            def save_qT(s):
                sp.wait_ge(qT_hi_ready, s + 1)
                for h in range(EH):
                    sp.dma_start(qT_w[s, h, 0], qT_hi[:, h, :, :].bitcast(fp32)).then_inc(qT_saved, 16)
                sp.wait_ge(qT_lo_ready, s + 1)
                for h in range(EH):
                    sp.dma_start(qT_w[s, h, 1], qT_lo[:, h, :, :].bitcast(fp32)).then_inc(qT_saved, 16)

            def load_stack(g, b, s_done):
                sp.dma_start(keys[b][0:32, :].bitcast(fp32).rearrange("p (h n) -> p h n", h=EH), qT_r[g]).then_inc(s_done, 16)
                sp.dma_start(keys[b][32:64, :].bitcast(fp32).rearrange("p (h n) -> p h n", h=EH), qT_r[g]).then_inc(s_done, 16)
                sp.dma_start(queries[b][0:32, :].bitcast(fp32).rearrange("p (h n) -> p h n", h=EH), qT_r[g]).then_inc(s_done, 16)
                sp.dma_start(queries[b][32:48, :].bitcast(fp32).rearrange("p (h n) -> p h n", h=EH), qT_r[g, 16:32]).then_inc(s_done, 16)
                sp.dma_start(queries[b][48:64, :].bitcast(fp32).rearrange("p (h n) -> p h n", h=EH), qT_r[g, 0:16]).then_inc(s_done, 16)

            def first_phase(s):
                if not (isinstance(s, int) and s == SETS - 1):
                    load_x(s + 1)
                save_qT(s)

            load_x(0)
            sp.dma_start(bq_b[:, :], bq[None, :].to_broadcast([P, EMB])).then_inc(small_loaded, 16)
            sp.dma_start(b2_b[:, :], fc2_bias[None, :].to_broadcast([P, EMB])).then_inc(small_loaded, 16)
            sp.dma_start(wq_sb[:, :, :], wqT.rearrange("(k p) n -> p k n", p=P)).then_inc(small_loaded, 16)
            sp.dma_start(st1.rearrange("p (k n) -> p k n", k=EH), fc1_q.rearrange("(k p) n -> p k n", p=P)).then_inc(w1_loaded, 16)
            for k in range(EH):
                sp.dma_start(st1s[:, k * F:(k + 1) * F], fc1_scales[k:k + 1, :].to_broadcast([P, F])).then_inc(w1_loaded, 16)
            sp.dma_start(st2.rearrange("p (k n) -> p k n", k=FC), fc2_q.rearrange("(k p) n -> p k n", p=P)).then_inc(w2_loaded, 16)
            for k in range(FC):
                sp.dma_start(st2s[:, k * EMB:(k + 1) * EMB], fc2_scales[k:k + 1, :].to_broadcast([P, EMB])).then_inc(w2_loaded, 16)
            sp.dma_start(bu_b[:, :], bu[None, :].to_broadcast([P, EMB])).then_inc(wu_loaded, 16)
            sp.dma_start(wu_sb[:, :, :], wuT.rearrange("(k p) n -> p k n", p=P)).then_inc(wu_loaded, 16)
            all_sets(sp, first_phase)

            sp.wait_ge(qT_saved, SETS * 2 * EH * 16)
            sp.wait_ge(consts_ready, 1)
            sp.wait_ge(flag_ready, 1)
            wide = sp.value_load(flag[0:1, 0:1])
            with sp.If(wide):
                load_stack(0, 0, gen_loaded)
                with sp.Fori(1, GROUPS) as g:
                    sp.wait_ge(gen_scored, g * (2 * CH))
                    load_stack(g, 0, gen_loaded)
                sp.wait_ge(gen_scored, GROUPS * 2 * CH)

            for g in range(NB):
                load_stack(g, g, stack_loaded[g])
            sp.wait_ge(neg_ready, 2)
            sp.dma_start(sh_w[0], neg_hi.bitcast(fp32).rearrange("p (b r) -> p b r", b=4)).then_inc(shift_saved, 16)
            sp.dma_start(sh_w[1], neg_lo.bitcast(fp32).rearrange("p (b r) -> p b r", b=4)).then_inc(shift_saved, 16)
            sp.wait_ge(shift_saved, 32)
            for g in range(NB):
                sp.dma_start(queries[g][64:66, :].bitcast(fp32), sh_r[g]).then_inc(stack_loaded[g], 16)
            sp.wait_ge(xn_ready, SETS)

            def attention(g, u, first, last):
                sp.dma_start(x_re[u % 2], x_grp[g]).then_inc(x_reloaded[u % 2], 16)
                if not last:
                    sp.wait_ge(scored, (g + 1) * (2 * NQ))
                    load_stack(g + NB, u % NB, stack_loaded[u % NB])
                    sp.dma_start(queries[u % NB][64:66, :].bitcast(fp32), sh_r[g + NB]).then_inc(stack_loaded[u % NB], 16)
                if not first:
                    sp.wait_ge(res_ready, g)
                    sp.dma_start(out_grp[g - 1], res[(u + 1) % 2]).then_inc(stored[(u + 1) % 2], 16)

            def attention_all():
                attention(0, 0, True, False)
                with sp.Fori(0, (GROUPS - 2) // 6 - 1) as i:
                    for u in range(6):
                        attention(i * 6 + (u + 1), (u + 1) % 6, False, False)
                for g in range(GROUPS - 7, GROUPS):
                    attention(g, g % 6, False, g + NB >= GROUPS)

            attention_all()
            sp.wait_ge(res_ready, GROUPS)
            sp.dma_start(out_grp[GROUPS - 1], res[(GROUPS - 1) % 2]).then_inc(stored[(GROUPS - 1) % 2], 16)
            for b in range(2):
                sp.wait_ge(stored[b], 16 * GROUPS // 2)

        @block.gpsimd
        def _(pool):
            pool.dma_start(b1_c[:, :], fc1_bias).then_inc(columns_loaded, 16)
            pool.dma_start(gamma_c[:, :], ln_gamma).then_inc(columns_loaded, 16)
            pool.dma_start(beta_c[:, :], ln_beta).then_inc(columns_loaded, 16)
            pool.memset(ident[:, :], 0.0).then_inc(pool_step, 1)
            pool.wait_ge(pool_step, 1)
            pool.affine_select(out=ident[:, :], in_=ident[:, :], compare_op=ALU.not_equal, fill=1.0,
                               base=0, pattern=[[-1, P]], channel_multiplier=1).then_inc(pool_step, 1)
            pool.memset(ones_row[:, :], 1.0).then_inc(pool_step, 1)

            def seed_gate(s):
                after(pool, xn_ready, s + 1)
                pool.tensor_tensor(gate[:, bass.ds(s * (GPS * EMB), GPS * EMB)].rearrange("p (g e) -> p g e", g=GPS),
                                   xn[:, :, :], b2_b[:, :].unsqueeze(1).to_broadcast([P, GPS, EMB]),
                                   ALU.add).then_inc(gate_seeded, 1)

            def first_phase(s):
                after(pool, q_tile_ready, s + 1)
                after(pool, norm2_ready, s)
                pool.tensor_tensor(q_sq[:, :], q_tile[:, :, :].rearrange("p g e -> p (g e)"),
                                   q_tile[:, :, :].rearrange("p g e -> p (g e)"), ALU.mult).then_inc(q_sq_ready, 1)
                pool.tensor_copy(q_rows[:, bass.ds(s * (GPS * EMB), GPS * EMB)],
                                 q_tile[:, :, :].rearrange("p g e -> p (g e)")).then_inc(q_rows_saved, 1)
                if not (isinstance(s, int) and s == SETS - 1):
                    seed_gate(s + 1)

            pool.wait_ge(b2_halved, 1)
            seed_gate(0)
            for b in range(NB):
                pool.memset(keys[b][:, :].bitcast(fp32), 0.0)
                pool.memset(queries[b][:, :].bitcast(fp32), 0.0)
                pool.memset(values[b][:, :, :], 0.0)
            pool.memset(nmax[:, :], 0.0).then_inc(pool_step, 1)
            pool.wait_ge(pool_step, 4)
            for b in range(NB):
                last = pool.memset(values[b][:, :, HD:HD + 1], 1.0)
            last.then_inc(pool_step, 1)
            pool.wait_ge(pool_step, 5)
            for b in range(NB):
                last = pool.memset(keys[b][64:66, :].bitcast(fp32), 1.0)
            last.then_inc(consts_ready, 1)
            pool.wait_ge(consts_ready, 1)
            pool.wait_ge(w1_ready, 1)
            pool.wait_ge(w2_ready, 1)
            all_sets(pool, first_phase)

            def build_values(g, b):
                after(pool, pv_done, (g - (NB - 1)) * NQ)
                pool.tensor_copy(values[b][:, :, 0:HD].rearrange("p (h c) d -> p h c d", h=EH),
                                 q_rows[:, bass.ds(g * EMB, EMB)].rearrange("p (h d c) -> p h c d", h=EH, d=HD))\
                    .then_inc(values_ready, 1)

            def finish(g, b, n):
                pool.wait_ge(s_ready, n)
                after(pool, stored[b], (g - b) * 8)
                pool.tensor_tensor(res[b], s_sb[b], gate[:, bass.ds(g * EMB, EMB)], ALU.mult).then_inc(gated, 1)
                pool.wait_ge(gated, n + 1)
                pool.wait_ge(x_reloaded[b], (g - b) * 8 + 16)
                pool.tensor_tensor(res[b], res[b], x_re[b], ALU.add).then_inc(res_ready, 1)

            pool.wait_ge(gate_ready, SETS)
            pool.wait_ge(hn_ready, SETS)
            pool.wait_ge(q_rows_saved, SETS)
            build_values(0, 0)
            build_values(1, 1)
            pool.sem_inc(gated, 1)

            def steady(g, u, first, last):
                if not last:
                    if not (isinstance(g, int) and g + 2 >= GROUPS):
                        build_values(g + 2, (u + 2) % NB)
                if not first:
                    finish(g - 1, (u + 1) % 2, g)

            for g in range(3):
                steady(g, g % 6, g == 0, False)
            with pool.Fori(0, (GROUPS - 2) // 6 - 1) as i:
                for u in range(6):
                    steady(i * 6 + (u + 3), (u + 3) % 6, False, False)
            for g in range(GROUPS - 5, GROUPS):
                steady(g, g % 6, False, False)
            finish(GROUPS - 1, (GROUPS - 1) % 2, GROUPS)

        @block.scalar
        def _(act):
            def turn_xn(s):
                act.wait_ge(xnT_in_psum, s + 1)
                act.activation(xnT[:, :], PA[:, :], ACT.Copy).then_inc(xnT_ready, 1)

            def deviations(s, n):
                act.wait_ge(var_ready, s * 2 + (n + 1))
                act.activation(sd[:, :], ve[:, :], ACT.Sqrt).then_inc(sd_ready, 1)

            def silu_gate(s):
                act.wait_ge(z_added, s + 1)
                part = gate[:, bass.ds(s * (GPS * EMB), GPS * EMB)]
                act.activation(part, part, ACT.Silu).then_inc(gate_ready, 1)

            def first_phase(s):
                last = isinstance(s, int) and s == SETS - 1
                if not (isinstance(s, int) and s == 0):
                    silu_gate(s - 1)
                act.wait_ge(qT_in_psum, s + 1)
                after(act, qT_saved, s * (2 * EH * 16))
                act.activation(qT_hi[:, :, :, :].rearrange("p h g r -> p (h g r)"), PB[:, :], ACT.Copy)\
                    .then_inc(qT_hi_ready, 1)
                for f in range(FC):
                    act.wait_ge(fc1_in_psum, s * FC + (f + 1))
                    if f == 0:
                        after(act, fc2_in_psum, s)
                    act.activation(yT[:, f, :], PC[:, (f % 2) * QT:(f % 2 + 1) * QT], ACT.Silu,
                                   bias=b1_c[:, f:f + 1]).then_inc(y_ready, 1)
                    if not last and f in (1, 4):
                        deviations(s + 1, f // 4)
                if not last:
                    turn_xn(s + 1)

            deviations(0, 0)
            deviations(0, 1)
            turn_xn(0)
            act.wait_ge(small_loaded, 48)
            act.wait_ge(columns_loaded, 48)
            all_sets(act, first_phase)
            silu_gate(SETS - 1)

            def attention(g, u, first, last):
                for n in range(NQ):
                    for h in range(2):
                        half = u * 2 * NQ + 2 * n + h
                        act.wait_ge(scored, g * (2 * NQ) + (2 * n + h + 1))
                        if h == 0:
                            after(act, pv_done, g * NQ + (n - (NB - 1)))
                        at = ((u * NQ + n) % NB) * 4 * QT + h * 2 * QT
                        act.activation(ring[:, at:at + 2 * QT], score_ps[half % NB][:, :], ACT.Exp,
                                       scale=SCALE).then_inc(exped, 1)

            act.wait_ge(fc2_in_psum, SETS)
            all_groups(act, attention)

        @block.vector
        def _(dve):
            def layer_norm(s):
                step = [0]

                def link(ins):
                    step[0] += 1
                    ins.then_inc(ln_step, 1)
                    dve.wait_ge(ln_step, s * LN_STEPS + step[0])

                dve.wait_ge(x_loaded, s * 16 + 16)
                for n, (src, dst, done) in enumerate(((x_in, xn, xn_ready), (xn, hn, hn_ready))):
                    for g in range(GPS):
                        last = dve.bn_stats(stats[:, g, :], src[:, g, :])
                    link(last)
                    dve.tensor_tensor(mu[:, :], stats[:, :, 1], stats[:, :, 4], ALU.add)
                    dve.tensor_tensor(nt[:, :], stats[:, :, 1], stats[:, :, 4], ALU.subtract)
                    link(dve.tensor_tensor(ve[:, :], stats[:, :, 2], stats[:, :, 5], ALU.add))
                    dve.tensor_scalar(mu[:, :], mu[:, :], 0.5, None, ALU.mult)
                    dve.scalar_tensor_tensor(out=nt[:, :], in0=nt[:, :], scalar=0.25, in1=nt[:, :],
                                             op0=ALU.mult, op1=ALU.mult)
                    link(dve.tensor_scalar(ve[:, :], ve[:, :], 1.0 / EMB, EPS, ALU.mult, ALU.add))
                    dve.tensor_tensor(ve[:, :], ve[:, :], nt[:, :], ALU.add).then_inc(var_ready, 1)
                    dve.wait_ge(sd_ready, s * 2 + (n + 1))
                    link(dve.reciprocal(rs[:, :], sd[:, :]))
                    link(dve.tensor_tensor(nt[:, :], rs[:, :], rs[:, :], ALU.mult))
                    link(dve.tensor_tensor(nt[:, :], nt[:, :], ve[:, :], ALU.mult))
                    link(dve.tensor_scalar(nt[:, :], nt[:, :], -0.5, 1.5, ALU.mult, ALU.add))
                    link(dve.tensor_tensor(rs[:, :], rs[:, :], nt[:, :], ALU.mult))
                    if n == 0:
                        after(dve, xnT_in_psum, s)
                        after(dve, hT_in_psum, s)
                        after(dve, gate_seeded, s)
                    for g in range(GPS):
                        last = dve.tensor_scalar(dst[:, g, :], src[:, g, :], mu[:, g:g + 1], rs[:, g:g + 1],
                                                 ALU.subtract, ALU.mult)
                    last.then_inc(done, 1)
                    if n == 0:
                        dve.wait_ge(xn_ready, s + 1)
                assert step[0] == LN_STEPS

            def turn_h(s):
                dve.wait_ge(hT_in_psum, s + 1)
                for h in range(EH):
                    last = dve.tensor_scalar(hT[:, h * SR:(h + 1) * SR], PB[:, h * SR:(h + 1) * SR],
                                             gamma_c[:, h:h + 1], beta_c[:, h:h + 1], ALU.mult, ALU.add)
                last.then_inc(hT_ready, 1)

            def add_z(s):
                dve.wait_ge(fc2_in_psum, s + 1)
                dve.wait_ge(gate_seeded, s + 1)
                part = gate[:, bass.ds(s * (GPS * EMB), GPS * EMB)]
                dve.scalar_tensor_tensor(out=part, in0=PD[:, :], scalar=0.5, in1=part, op0=ALU.mult, op1=ALU.add)\
                    .then_inc(z_added, 1)

            def first_phase(s):
                if not (isinstance(s, int) and s == 0):
                    add_z(s - 1)
                dve.wait_ge(q_in_psum, s + 1)
                after(dve, q_sq_ready, s)
                after(dve, q_rows_saved, s)
                after(dve, qT_in_psum, s)
                dve.tensor_tensor(q_tile[:, :, :], PA[:, :].rearrange("p (g e) -> p g e", g=GPS),
                                  bq_b[:, :].unsqueeze(1).to_broadcast([P, GPS, EMB]), ALU.add)\
                    .then_inc(q_tile_ready, 1)
                dve.wait_ge(qT_hi_ready, s + 1)
                after(dve, qT_saved, s * (2 * EH * 16))
                dve.tensor_tensor(qT_lo[:, :, :, :].rearrange("p h g r -> p (h g r)"), PB[:, :],
                                  qT_hi[:, :, :, :].rearrange("p h g r -> p (h g r)").bitcast(fp32),
                                  ALU.subtract).then_inc(qT_lo_ready, 1)
                dve.wait_ge(q_sq_ready, s + 1)
                dve.tensor_reduce(norm2[:, bass.ds(s * (GPS * CH), GPS * CH)].rearrange("p (t c) -> p t c", c=CH // EH),
                                  q_sq[:, :].rearrange("p (t d c) -> p t c d", d=HD, c=CH // EH), AX.X, ALU.add)\
                    .then_inc(norm2_ready, 1)
                if not (isinstance(s, int) and s == SETS - 1):
                    layer_norm(s + 1)
                    turn_h(s + 1)

            dve.wait_ge(small_loaded, 48)
            dve.wait_ge(columns_loaded, 48)
            dve.tensor_scalar(b2_b[:, :], b2_b[:, :], 0.5, None, ALU.mult).then_inc(b2_halved, 1)
            layer_norm(0)
            turn_h(0)
            dve.wait_ge(w1_loaded, 16 * (1 + EH))
            dve.scalar_tensor_tensor(out=w1.rearrange("p k n -> p (k n)"), in0=st1, scalar=-128.0, in1=st1s,
                                     op0=ALU.add, op1=ALU.mult).then_inc(w1_ready, 1)
            dve.wait_ge(w2_loaded, 16 * (1 + FC))
            dve.scalar_tensor_tensor(out=w2[:, :, :].rearrange("p k n -> p (k n)"), in0=st2, scalar=-128.0, in1=st2s,
                                     op0=ALU.add, op1=ALU.mult).then_inc(w2_ready, 1)
            all_sets(dve, first_phase)

            dve.wait_ge(norm2_ready, SETS)
            dve.wait_ge(pool_step, 4)
            dve.tensor_reduce(nmax[:, :], norm2[:, :], AX.X, ALU.max).then_inc(shift_step, 1)
            dve.wait_ge(shift_pe, 1)
            dve.tensor_reduce(top[:, :], PA[0:1, 0:P], AX.X, ALU.max).then_inc(shift_step, 1)
            dve.wait_ge(shift_step, 2)
            dve.tensor_scalar(flag[:, :], top[:, :], COMMON_MAX_LIMIT / SCALE, None, ALU.is_gt).then_inc(flag_ready, 1)
            dve.wait_ge(shift_pe, 2)
            dve.tensor_copy(nmax[:, :], PA[:, QT:QT + 1]).then_inc(shift_step, 1)
            dve.wait_ge(shift_step, 3)
            dve.tensor_scalar(shift[:, :], norm2[:, :], nmax[:, 0:1], None, ALU.max).then_inc(shift_step, 1)
            dve.wait_ge(flag_ready, 1)
            wide = dve.value_load(flag[0:1, 0:1])
            with dve.If(wide):
                dve.wait_ge(norm2_ready, SETS)
                dve.wait_ge(shift_step, 4)
                dve.memset(q_sq[:, :], 0.0).then_inc(gen_reduced, 1)
                dve.wait_ge(gen_reduced, 1)
                with dve.Fori(0, GROUPS) as g:
                    for c in range(CH):
                        for h in range(2):
                            dve.wait_ge(gen_scored, g * (2 * CH) + (2 * c + h + 1))
                            dve.tensor_reduce(q_sq[:, bass.ds(g * (2 * CH) + (2 * c + h), 1)],
                                              [PA, PB][h][:, :], AX.X, ALU.max).then_inc(gen_reduced, 1)
                dve.wait_ge(gen_reduced, GROUPS * 2 * CH + 1)
                dve.tensor_reduce(shift[:, :], q_sq[:, :].rearrange("p (t h) -> p t h", h=2), AX.X, ALU.max)\
                    .then_inc(shift_step, 1)
                dve.wait_ge(shift_step, 5)
            dve.wait_ge(shift_step, 4)
            dve.tensor_copy(nmax[:, :], shift[:, 0:1]).then_inc(shift_ready, 1)
            dve.wait_ge(shift_pe, 3)
            dve.wait_ge(hT_in_psum, SETS)
            dve.wait_ge(qT_saved, SETS * 2 * EH * 16)
            dve.tensor_scalar(neg, PA[:, 0:QT], -1.0, None, ALU.mult).then_inc(neg_ready, 1)
            dve.tensor_scalar(neg_hi, PA[:, 0:QT], -1.0, None, ALU.mult).then_inc(shift_ready, 1)
            dve.wait_ge(neg_ready, 1)
            dve.wait_ge(shift_ready, 2)
            dve.tensor_tensor(neg_lo, neg, neg_hi.bitcast(fp32), ALU.subtract).then_inc(neg_ready, 1)
            add_z(SETS - 1)

            def tail(g, b, t, out_buf):
                n = g * TILES + (t + 1)
                dve.wait_ge(pv_done, g * NQ + (t + 1) * QUADS)
                dve.tensor_copy(acc_sb[t % 2], acc_ps[t % 2]).then_inc(acc_copied, 1)
                dve.wait_ge(acc_turned, n)
                dve.tensor_reduce(sums, acc_ps[t % 2].rearrange("p (c a m) -> p c m a", c=4, a=4)[:, :, 0:HD + 1, :],
                                  AX.X, ALU.add).then_inc(acc_summed, 1)
                dve.wait_ge(acc_summed, n)
                dve.reciprocal(rden, sums[:, :, HD]).then_inc(tail_step, 1)
                dve.wait_ge(tail_step, n)
                dve.tensor_tensor(out_buf[:, t * 4 * HD:(t + 1) * 4 * HD].rearrange("p (c d) -> p c d", c=4),
                                  sums[:, :, 0:HD], rden.unsqueeze(2).to_broadcast([P, 4, HD]), ALU.mult)\
                    .then_inc(attn_ready, 1)

            def project(g, b, n):
                dve.wait_ge(attnT_in_psum, n)
                dve.tensor_copy(attnT.rearrange("p h n -> p (h n)"), acc_ps[1][:, 0:EH * P]).then_inc(attnT_ready, 1)
                dve.wait_ge(s_in_psum, n)
                dve.wait_ge(gated, n)
                dve.tensor_tensor(s_sb[b], acc_ps[1][:, 0:EMB], bu_b[:, :], ALU.add).then_inc(s_ready, 1)

            def attention(g, u, first, last):
                if not first:
                    tail(g - 1, 0, TILES - 1, attn[(u + 1) % 2])
                    project(g - 1, (u + 1) % 2, g)
                for t in range(TILES - 1):
                    tail(g, 0, t, attn[u % 2])

            dve.wait_ge(wu_loaded, 32)
            dve.wait_ge(gate_seeded, SETS)
            all_groups(dve, attention)
            tail(GROUPS - 1, 0, TILES - 1, attn[(GROUPS - 1) % 2])
            project(GROUPS - 1, (GROUPS - 1) % 2, GROUPS)

        @block.tensor
        def _(pe):
            def turn(s):
                pe.wait_ge(xn_ready, s + 1)
                after(pe, q_tile_ready, s)
                for h in range(EH):
                    for g in range(GPS):
                        mm = pe.transpose(PA[:, h * SR + g * P:h * SR + (g + 1) * P],
                                          xn[:, g, h * P:(h + 1) * P], ident[:, :])
                mm.then_inc(xnT_in_psum, 1)
                pe.wait_ge(hn_ready, s + 1)
                after(pe, qT_lo_ready, s)
                for h in range(EH):
                    for g in range(GPS):
                        mm = pe.transpose(PB[:, h * SR + g * P:h * SR + (g + 1) * P],
                                          hn[:, g, h * P:(h + 1) * P], ident[:, :])
                mm.then_inc(hT_in_psum, 1)

            def fc1(s):
                pe.wait_ge(hT_ready, s + 1)
                for f in range(FC):
                    after(pe, y_ready, s * FC + (f - 1))
                    for k in range(EH):
                        mm = pe.matmul(PC[:, (f % 2) * QT:(f % 2 + 1) * QT], w1[:, k, f * P:(f + 1) * P],
                                       hT[:, k * SR:(k + 1) * SR], start=(k == 0), stop=(k == EH - 1))
                    mm.then_inc(fc1_in_psum, 1)

            def fc2(s):
                pe.wait_ge(y_ready, s * FC + FC)
                after(pe, z_added, s)
                for g in range(GPS):
                    for k in range(FC):
                        mm = pe.matmul(PD[:, g * FB:(g + 1) * FB], yT[:, k, g * P:(g + 1) * P], w2[:, k, :],
                                       start=(k == 0), stop=(k == FC - 1))
                mm.then_inc(fc2_in_psum, 1)

            def first_phase(s):
                pe.wait_ge(xnT_ready, s + 1)
                for g in range(GPS):
                    for k in range(EH):
                        mm = pe.matmul(PA[:, g * FB:(g + 1) * FB], xnT[:, k * SR + g * P:k * SR + (g + 1) * P],
                                       wq_sb[:, k, :], start=(k == 0), stop=(k == EH - 1))
                mm.then_inc(q_in_psum, 1)
                pe.wait_ge(q_tile_ready, s + 1)
                pe.wait_ge(hT_ready, s + 1)
                for h in range(EH):
                    for g in range(GPS):
                        mm = pe.transpose(PB[:, h * SR + g * P:h * SR + (g + 1) * P],
                                          q_tile[:, g, h * P:(h + 1) * P], ident[:, :])
                mm.then_inc(qT_in_psum, 1)
                if isinstance(s, int) and s == 0:
                    pe.wait_ge(w1_ready, 1)
                fc1(s)
                if isinstance(s, int) and s == SETS - 1:
                    make_shift()
                else:
                    turn(s + 1)
                if isinstance(s, int) and s == 0:
                    pe.wait_ge(w2_ready, 1)
                fc2(s)

            def make_shift():
                pe.wait_ge(shift_step, 1)
                pe.wait_ge(q_tile_ready, SETS)
                pe.transpose(PA[0:1, 0:P], nmax[:, 0:1], ident[:, :]).then_inc(shift_pe, 1)
                pe.wait_ge(shift_step, 2)
                pe.matmul(PA[:, QT:QT + 1], ones_row[0:1, :], top[0:1, 0:1], start=True, stop=True).then_inc(shift_pe, 1)
                pe.wait_ge(flag_ready, 1)
                wide = pe.value_load(flag[0:1, 0:1])
                with pe.If(wide):
                    pe.wait_ge(qT_lo_ready, SETS)
                    pe.wait_ge(shift_step, 4)
                    with pe.Fori(0, GROUPS) as g:
                        pe.wait_ge(gen_loaded, g * (GEN_DMAS * 16) + GEN_DMAS * 16)
                        for c in range(CH):
                            for h in range(2):
                                pe.wait_ge(gen_reduced, g * (2 * CH) + (2 * c + h + 1))
                                for j in range(2):
                                    mm = pe.matmul([PA, PB][h][:, j * QT:(j + 1) * QT], keys[0][:, c * P:(c + 1) * P],
                                                   queries[0][:, (2 * h + j) * QT:(2 * h + j + 1) * QT],
                                                   start=True, stop=True)
                                mm.then_inc(gen_scored, 1)
                pe.wait_ge(shift_ready, 1)
                for b in range(4):
                    mm = pe.transpose(PA[:, b * P:(b + 1) * P], shift[:, b * P:(b + 1) * P], ident[:, :])
                mm.then_inc(shift_pe, 1)

            pe.wait_ge(pool_step, 3)
            turn(0)
            pe.wait_ge(small_loaded, 48)
            pe.wait_ge(columns_loaded, 48)
            all_sets(pe, first_phase)

            def scores(g, u, n):
                t, k = n // QUADS, n % QUADS
                if n == 0:
                    pe.wait_ge(stack_loaded[u % NB], stack_count(g, u % NB))
                for h in range(2):
                    half = u * 2 * NQ + 2 * n + h
                    after(pe, exped, g * (2 * NQ) + (2 * n + h - (NB - 1)))
                    for j in range(2):
                        c = 4 * k + 2 * h + j
                        mm = pe.matmul(score_ps[half % NB][:, j * QT:(j + 1) * QT], keys[u % NB][:, c * P:(c + 1) * P],
                                       queries[u % NB][:, t * QT:(t + 1) * QT], start=True, stop=True)
                    mm.then_inc(scored, 1)

            def stack_count(g, b):
                return (g - b) * (STACK_DMAS * 16 // NB) + STACK_DMAS * 16

            def weigh(g, u, n):
                t, k = n // QUADS, n % QUADS
                if n == 0:
                    pe.wait_ge(values_ready, g + 1)
                if k == 0:
                    after(pe, acc_summed, g * TILES + (t - 1))
                    if t == 1:
                        after(pe, s_ready, g)
                pe.wait_ge(exped, g * (2 * NQ) + (2 * n + 2))
                at = ((u * NQ + n) % NB) * 4 * QT
                for a in range(4):
                    mm = pe.matmul(acc_ps[t % 2][a * VW:(a + 1) * VW, :], values[u % NB][:, 4 * k + a, :],
                                   ring[:, at + a * QT:at + (a + 1) * QT], start=(k == 0), stop=(k == QUADS - 1),
                                   skip_group_check=True)
                mm.then_inc(pv_done, 1)

            def turn_acc(g, t):
                pe.wait_ge(acc_copied, g * TILES + (t + 1))
                for c in range(4):
                    mm = pe.transpose(acc_ps[t % 2][:, c * P:(c + 1) * P], acc_sb[t % 2][:, c * P:(c + 1) * P], ident[:, :])
                mm.then_inc(acc_turned, 1)

            def turn_attn(g, u):
                pe.wait_ge(attn_ready, g * TILES + TILES)
                for h in range(EH):
                    mm = pe.transpose(acc_ps[1][:, h * P:(h + 1) * P], attn[u % 2][:, h * P:(h + 1) * P], ident[:, :])
                mm.then_inc(attnT_in_psum, 1)

            def project(g):
                pe.wait_ge(attnT_ready, g + 1)
                for h in range(EH):
                    mm = pe.matmul(acc_ps[1][:, 0:EMB], attnT[:, h, :], wu_sb[:, h, :], start=(h == 0), stop=(h == EH - 1))
                mm.then_inc(s_in_psum, 1)

            def attention(g, u, first, last):
                for n in range(NQ):
                    if n + 1 < NQ:
                        scores(g, u, n + 1)
                    elif not last:
                        scores(g + 1, (u + 1) % 6, 0)
                    weigh(g, u, n)
                    if n % QUADS == 0 and n > 0:
                        turn_acc(g, n // QUADS - 1)
                    if not first:
                        if n == 0:
                            turn_acc(g - 1, TILES - 1)
                        if n == 1:
                            turn_attn(g - 1, (u + 1) % 2)
                        if n == 2:
                            project(g - 1)

            pe.wait_ge(shift_pe, 3)
            pe.wait_ge(y_ready, SETS * FC)
            pe.wait_ge(z_added, SETS)
            pe.wait_ge(neg_ready, 2)
            pe.wait_ge(qT_lo_ready, SETS)
            pe.wait_ge(wu_loaded, 32)
            scores(0, 0, 0)
            all_groups(pe, attention)
            turn_acc(GROUPS - 1, TILES - 1)
            turn_attn(GROUPS - 1, (GROUPS - 1) % 2)
            project(GROUPS - 1)


_INS = ["x", "wqT", "bq", "wuT", "bu", "ln_gamma", "ln_beta", "fc1_q", "fc1_scales", "fc1_bias",
        "fc2_q", "fc2_scales", "fc2_bias"]


def kernel(L0_attn_x, L0_attn_wq, L0_attn_bq, L0_attn_wu, L0_attn_bu, L0_ffn_ln_gamma, L0_ffn_ln_beta,
           L0_ffn_fc1_q, L0_ffn_fc1_scales, L0_ffn_fc1_bias, L0_ffn_fc2_q, L0_ffn_fc2_scales, L0_ffn_fc2_bias):
    import numpy as np
    import concourse.bacc as bacc
    from concourse import mybir as mb
    from concourse.bass_utils import run_bass_kernel_spmd as run

    def columns(a):
        return np.asarray(a).reshape(-1, 128).T

    def by_place(a):
        a = np.asarray(a)
        return a.reshape(a.shape[:-1] + (2, 8, 16)).swapaxes(-1, -2).reshape(a.shape)

    shape = L0_attn_x.shape
    rows = shape[0] * shape[1]
    arrays = [np.asarray(L0_attn_x).reshape(rows, shape[2]), by_place(np.asarray(L0_attn_wq).T), by_place(L0_attn_bq),
              np.asarray(L0_attn_wu).T, L0_attn_bu, columns(L0_ffn_ln_gamma), columns(L0_ffn_ln_beta), L0_ffn_fc1_q,
              L0_ffn_fc1_scales, columns(L0_ffn_fc1_bias), L0_ffn_fc2_q, L0_ffn_fc2_scales, L0_ffn_fc2_bias]
    nc = bacc.Bacc("TRN2", target_bir_lowering=False, num_devices=1)
    ins, args = {}, []
    for name, a in zip(_INS, arrays):
        a = np.ascontiguousarray(a)
        ins[f"in_{name}"] = a
        args.append(nc.dram_tensor(f"in_{name}", a.shape, mb.dt.from_np(a.dtype), kind="ExternalInput").ap())
    args.append(nc.dram_tensor("out_rows", (rows, shape[2]), mb.dt.float32, kind="ExternalOutput").ap())
    groups = rows // 128
    args.append(nc.dram_tensor("qT_scratch", (groups, 2, 2, 16, 1024), mb.dt.float32, kind="Internal").ap())
    args.append(nc.dram_tensor("shift_scratch", (2, groups * 16, 128), mb.dt.float32, kind="Internal").ap())
    attention_times_ffn_gate(nc, *args)
    r = run(nc, [ins], core_ids=[0])
    return r.results[0]["out_rows"].reshape(shape)
```

```python
import concourse.bass as bass
from concourse import mybir
from contextlib import ExitStack

COMMON_MAX_LIMIT = 60.0


def attention_times_ffn_gate(
    nc: bass.Bass,
    x: bass.AP,
    wqT: bass.AP,
    bq: bass.AP,
    wuT: bass.AP,
    bu: bass.AP,
    ln_gamma: bass.AP,
    ln_beta: bass.AP,
    fc1_q: bass.AP,
    fc1_scales: bass.AP,
    fc1_bias: bass.AP,
    fc2_q: bass.AP,
    fc2_scales: bass.AP,
    fc2_bias: bass.AP,
    out: bass.AP,
    qT_scratch: bass.AP,
    shift_scratch: bass.AP,
):
    fp32 = mybir.dt.float32
    f32r = mybir.dt.float32r
    i32 = mybir.dt.int32
    ALU = mybir.AluOpType
    ACT = mybir.ActivationFunctionType
    AX = mybir.AxisListType

    P = 128
    ROWS, EMB = x.shape
    HD = 16
    CH = EMB // HD
    GROUPS = ROWS // P
    TOK = P * CH
    GPS = 4
    SETS = GROUPS // GPS
    SR = GPS * P
    EH = EMB // P
    F = fc1_q.shape[1]
    FC = F // P
    FB = EMB
    EPS = 1e-5
    SCALE = float(EMB) ** -0.5
    LN_STEPS = 30

    NB = 3
    QT = 512
    QS = TOK // QT
    VW = 32
    STACK_DMAS = 6
    GEN_DMAS = 5

    x_set = x.rearrange("(s g r) e -> s r g e", g=GPS, r=P)
    x_grp = x.rearrange("(g r) e -> g r e", r=P)
    out_grp = out.rearrange("(g r) e -> g r e", r=P)
    qT_w = qT_scratch.rearrange("(s g) h p d (c r) -> s h p (d c) g r", g=GPS, r=P)
    qT_r = qT_scratch.rearrange("g h p d n -> g (p d) h n")
    sh_w = shift_scratch.rearrange("p (b k) r -> p k b r", k=P)
    sh_r = shift_scratch.rearrange("p (g c) r -> g p (c r)", c=CH)

    ctx = ExitStack()
    with ctx:
        def sb(name, shape, dt=fp32):
            return ctx.enter_context(nc.sbuf_tensor(name, shape, dt))

        def sem(name):
            return ctx.enter_context(nc.semaphore(name))

        q_rows = sb("q_rows", [P, GROUPS * EMB])
        gate = sb("gate", [P, GROUPS * EMB])
        ring = sb("ring", [P, NB * QS * QT])
        keys = [sb("keys0", [P, TOK], f32r)]
        queries = [sb("queries0", [P, TOK], f32r)]
        with ExitStack() as ffn:
            w1_hi = ffn.enter_context(nc.sbuf_tensor("w1_hi", [P, EH, F], f32r))
            w1_lo = ffn.enter_context(nc.sbuf_tensor("w1_lo", [P, EH, F], f32r))
            hT_hi = ffn.enter_context(nc.sbuf_tensor("hT_hi", [P, EH * SR], f32r))
            hT_lo = ffn.enter_context(nc.sbuf_tensor("hT_lo", [P, EH * SR], f32r))
            y_more = ffn.enter_context(nc.sbuf_tensor("y_more", [P, 4, SR], fp32))
        keys += [sb(f"keys{b}", [P, TOK], f32r) for b in range(1, NB)]
        queries += [sb(f"queries{b}", [P, TOK], f32r) for b in range(1, NB)]
        with ExitStack() as ffn:
            y_part = ffn.enter_context(nc.sbuf_tensor("y_part", [P, SR], fp32))
            y_sum = ffn.enter_context(nc.sbuf_tensor("y_sum", [P, SR], fp32))
        values = [sb(f"values{b}", [P, CH, VW]) for b in range(NB)]
        w2 = sb("w2", [P, FC, EMB])
        wq_sb = sb("wq_sb", [P, EH, EMB])
        wu_sb = sb("wu_sb", [P, EH, EMB])
        bq_b = sb("bq_b", [P, EMB])
        bu_b = sb("bu_b", [P, EMB])
        b2_b = sb("b2_b", [P, EMB])
        b1_c = sb("b1_c", [P, FC])
        s1_c = sb("s1_c", [P, FC, EH])
        low_max = sb("low_max", [P, 1])
        low_top = sb("low_top", [1, 1])
        w_flag = sb("w_flag", [1, 1], i32)
        gamma_c = sb("gamma_c", [P, EH])
        beta_c = sb("beta_c", [P, EH])
        ident = sb("ident", [P, P])
        ones_row = sb("ones_row", [1, P])
        x_in = sb("x_in", [P, GPS, EMB])
        xn = sb("xn", [P, GPS, EMB])
        hn = sb("hn", [P, GPS, EMB])
        xnT = sb("xnT", [P, EH * SR])
        hT = sb("hT", [P, EH * SR])
        q_tile = sb("q_tile", [P, GPS, EMB])
        q_sq = sb("q_sq", [P, GPS * EMB])
        qT_hi = sb("qT_hi", [P, EH, GPS, P], f32r)
        qT_lo = sb("qT_lo", [P, EH, GPS, P], f32r)
        stats = sb("stats", [P, GPS, 6])
        mu = sb("mu", [P, GPS])
        ve = sb("ve", [P, GPS])
        rs = sb("rs", [P, GPS])
        nt = sb("nt", [P, GPS])
        norm2 = sb("norm2", [P, GROUPS * CH])
        shift = sb("shift", [P, GROUPS * CH])
        nmax = sb("nmax", [P, 1])
        top = sb("top", [1, 1])
        flag = sb("flag", [1, 1], i32)

        y_tiles = [y_more[:, f, :] for f in range(4)] + [ring[:, f * SR:(f + 1) * SR] for f in range(2 * FC - 4)]
        yT = [y_tiles[:FC], y_tiles[FC:]]
        st1 = q_rows[:, 0:EH * F].bitcast(i32)
        st1f = q_rows[:, EH * F:2 * EH * F]
        st2 = q_rows[:, 2 * EH * F:3 * EH * F].bitcast(i32)
        st2s = q_rows[:, 3 * EH * F:4 * EH * F]
        acc_sb = xnT[:, 0:QT]
        x_re = [x_in[:, 0, :], x_in[:, 1, :]]
        attn = [x_in[:, 2, :], x_in[:, 3, :]]
        attnT = hT[:, 0:EH * P].rearrange("p (h n) -> p h n", h=EH)
        s_sb = [xn[:, 0, :], xn[:, 1, :]]
        res = [xn[:, 2, :], xn[:, 3, :]]
        rden = hn[:, 0, 0:CH].rearrange("p (c q) -> p c q", c=CH // QS)
        neg = hn[:, 2:4, :].rearrange("p a b -> p (a b)")
        neg_hi = qT_hi[:, 0, :, :].rearrange("p a b -> p (a b)")
        neg_lo = qT_lo[:, 0, :, :].rearrange("p a b -> p (a b)")

        PA, PB, PC, PD = [ctx.enter_context(nc.psum_tensor(f"pair{i}", [P, 2 * QT], fp32)) for i in range(4)]
        score_ps = [PA, PB, PC]
        fc1_ps = [PC, PC, PB, PC, PB, PC, PB, PC]
        acc_ps = [PD[:, 0:QT], PD[:, QT:2 * QT]]

        x_loaded = sem("x_loaded")
        small_loaded = sem("small_loaded")
        columns_loaded = sem("columns_loaded")
        w1_loaded = sem("w1_loaded")
        w2_loaded = sem("w2_loaded")
        wu_loaded = sem("wu_loaded")
        w1_ready = sem("w1_ready")
        w2_ready = sem("w2_ready")
        b2_halved = sem("b2_halved")
        consts_ready = sem("consts_ready")
        pool_step = sem("pool_step")
        ln_step = sem("ln_step")
        xn_ready = sem("xn_ready")
        hn_ready = sem("hn_ready")
        gate_seeded = sem("gate_seeded")
        xnT_in_psum = sem("xnT_in_psum")
        hT_in_psum = sem("hT_in_psum")
        xnT_ready = sem("xnT_ready")
        hT_ready = sem("hT_ready")
        q_in_psum = sem("q_in_psum")
        q_tile_ready = sem("q_tile_ready")
        q_rows_saved = sem("q_rows_saved")
        q_sq_ready = sem("q_sq_ready")
        norm2_ready = sem("norm2_ready")
        qT_in_psum = sem("qT_in_psum")
        qT_hi_ready = sem("qT_hi_ready")
        qT_lo_ready = sem("qT_lo_ready")
        qT_saved = sem("qT_saved")
        fc1_in_psum = sem("fc1_in_psum")
        y_part_ready = sem("y_part_ready")
        y_sum_ready = sem("y_sum_ready")
        y_ready = sem("y_ready")
        hT_hi_ready = sem("hT_hi_ready")
        hT_lo_ready = sem("hT_lo_ready")
        w_step = sem("w_step")
        low_top_ready = sem("low_top_ready")
        low_in_psum = sem("low_in_psum")
        w_flag_ready = sem("w_flag_ready")
        late_consts = sem("late_consts")
        fc2_in_psum = sem("fc2_in_psum")
        z_added = sem("z_added")
        gate_ready = sem("gate_ready")
        shift_step = sem("shift_step")
        shift_pe = sem("shift_pe")
        flag_ready = sem("flag_ready")
        shift_ready = sem("shift_ready")
        neg_ready = sem("neg_ready")
        shift_saved = sem("shift_saved")
        gen_loaded = sem("gen_loaded")
        gen_scored = sem("gen_scored")
        gen_reduced = sem("gen_reduced")
        stack_loaded = [sem(f"stack_loaded{b}") for b in range(NB)]
        x_reloaded = [sem(f"x_reloaded{b}") for b in range(2)]
        values_ready = sem("values_ready")
        scored = sem("scored")
        exped = sem("exped")
        pv_done = sem("pv_done")
        acc_copied = sem("acc_copied")
        acc_turned = sem("acc_turned")
        rden_ready = sem("rden_ready")
        attn_ready = sem("attn_ready")
        attnT_in_psum = sem("attnT_in_psum")
        attnT_ready = sem("attnT_ready")
        s_in_psum = sem("s_in_psum")
        s_ready = sem("s_ready")
        gated = sem("gated")
        res_ready = sem("res_ready")
        stored = [sem(f"stored{b}") for b in range(2)]

        def after(eng, s, count):
            if not isinstance(count, int) or count > 0:
                eng.wait_ge(s, count)

        def all_sets(eng, step):
            step(0, 0, True, False)
            with eng.Fori(0, (SETS - 2) // 2) as i:
                step(i * 2 + 1, 1, False, False)
                step(i * 2 + 2, 0, False, False)
            step(SETS - 1, 1, False, True)

        def all_groups(eng, step):
            step(0, 0, True, False)
            with eng.Fori(0, (GROUPS - 2) // 6) as i:
                for u in range(6):
                    step(i * 6 + (u + 1), (u + 1) % 6, False, False)
            step(GROUPS - 1, (GROUPS - 1) % 6, False, True)

        block = ctx.enter_context(nc.Block())

        @block.sync
        def _(sp):
            def load_x(s):
                after(sp, xn_ready, s)
                sp.dma_start(x_in[:, :, :], x_set[s]).then_inc(x_loaded, 16)

            def save_qT(s):
                sp.wait_ge(qT_hi_ready, s + 1)
                for h in range(EH):
                    sp.dma_start(qT_w[s, h, 0], qT_hi[:, h, :, :].bitcast(fp32)).then_inc(qT_saved, 16)
                sp.wait_ge(qT_lo_ready, s + 1)
                for h in range(EH):
                    sp.dma_start(qT_w[s, h, 1], qT_lo[:, h, :, :].bitcast(fp32)).then_inc(qT_saved, 16)

            def load_stack(g, b, s_done):
                sp.dma_start(keys[b][0:32, :].bitcast(fp32).rearrange("p (h n) -> p h n", h=EH), qT_r[g]).then_inc(s_done, 16)
                sp.dma_start(keys[b][32:64, :].bitcast(fp32).rearrange("p (h n) -> p h n", h=EH), qT_r[g]).then_inc(s_done, 16)
                sp.dma_start(queries[b][0:32, :].bitcast(fp32).rearrange("p (h n) -> p h n", h=EH), qT_r[g]).then_inc(s_done, 16)
                sp.dma_start(queries[b][32:48, :].bitcast(fp32).rearrange("p (h n) -> p h n", h=EH), qT_r[g, 16:32]).then_inc(s_done, 16)
                sp.dma_start(queries[b][48:64, :].bitcast(fp32).rearrange("p (h n) -> p h n", h=EH), qT_r[g, 0:16]).then_inc(s_done, 16)

            def first_phase(s, odd, first, last):
                if not last:
                    load_x(s + 1)
                save_qT(s)

            load_x(0)
            sp.dma_start(st1.rearrange("p (k n) -> p k n", k=EH), fc1_q.rearrange("(k p) n -> p k n", p=P)).then_inc(w1_loaded, 16)
            sp.dma_start(bq_b[:, :], bq[None, :].to_broadcast([P, EMB])).then_inc(small_loaded, 16)
            sp.dma_start(b2_b[:, :], fc2_bias[None, :].to_broadcast([P, EMB])).then_inc(small_loaded, 16)
            sp.dma_start(wq_sb[:, :, :], wqT.rearrange("(k p) n -> p k n", p=P)).then_inc(small_loaded, 16)
            sp.dma_start(st2.rearrange("p (k n) -> p k n", k=FC), fc2_q.rearrange("(k p) n -> p k n", p=P)).then_inc(w2_loaded, 16)
            for k in range(FC):
                sp.dma_start(st2s[:, k * EMB:(k + 1) * EMB], fc2_scales[k:k + 1, :].to_broadcast([P, EMB])).then_inc(w2_loaded, 16)
            sp.dma_start(bu_b[:, :], bu[None, :].to_broadcast([P, EMB])).then_inc(wu_loaded, 16)
            sp.dma_start(wu_sb[:, :, :], wuT.rearrange("(k p) n -> p k n", p=P)).then_inc(wu_loaded, 16)
            all_sets(sp, first_phase)

            sp.wait_ge(qT_saved, SETS * 2 * EH * 16)
            sp.wait_ge(consts_ready, 1)
            sp.wait_ge(flag_ready, 1)
            wide = sp.value_load(flag[0:1, 0:1])
            with sp.If(wide):
                load_stack(0, 0, gen_loaded)
                with sp.Fori(1, GROUPS) as g:
                    sp.wait_ge(gen_scored, g * (2 * CH))
                    load_stack(g, 0, gen_loaded)
                sp.wait_ge(gen_scored, GROUPS * 2 * CH)

            load_stack(0, 0, stack_loaded[0])
            sp.wait_ge(neg_ready, 2)
            sp.dma_start(sh_w[0], neg_hi.bitcast(fp32).rearrange("p (b r) -> p b r", b=4)).then_inc(shift_saved, 16)
            sp.dma_start(sh_w[1], neg_lo.bitcast(fp32).rearrange("p (b r) -> p b r", b=4)).then_inc(shift_saved, 16)
            sp.wait_ge(shift_saved, 32)
            sp.dma_start(queries[0][64:66, :].bitcast(fp32), sh_r[0]).then_inc(stack_loaded[0], 16)
            sp.wait_ge(late_consts, 2)
            for g in range(1, NB):
                load_stack(g, g, stack_loaded[g])
                sp.dma_start(queries[g][64:66, :].bitcast(fp32), sh_r[g]).then_inc(stack_loaded[g], 16)
            sp.wait_ge(xn_ready, SETS)

            def attention(g, u, first, last):
                sp.dma_start(x_re[u % 2], x_grp[g]).then_inc(x_reloaded[u % 2], 16)
                if not last:
                    sp.wait_ge(scored, (g + 1) * (2 * CH))
                    load_stack(g + NB, u % NB, stack_loaded[u % NB])
                    sp.dma_start(queries[u % NB][64:66, :].bitcast(fp32), sh_r[g + NB]).then_inc(stack_loaded[u % NB], 16)
                if not first:
                    sp.wait_ge(res_ready, g)
                    sp.dma_start(out_grp[g - 1], res[(u + 1) % 2]).then_inc(stored[(u + 1) % 2], 16)

            def attention_all():
                attention(0, 0, True, False)
                with sp.Fori(0, (GROUPS - 2) // 6 - 1) as i:
                    for u in range(6):
                        attention(i * 6 + (u + 1), (u + 1) % 6, False, False)
                for g in range(GROUPS - 7, GROUPS):
                    attention(g, g % 6, False, g + NB >= GROUPS)

            attention_all()
            sp.wait_ge(res_ready, GROUPS)
            sp.dma_start(out_grp[GROUPS - 1], res[(GROUPS - 1) % 2]).then_inc(stored[(GROUPS - 1) % 2], 16)
            for b in range(2):
                sp.wait_ge(stored[b], 16 * GROUPS // 2)

        @block.gpsimd
        def _(pool):
            pool.dma_start(b1_c[:, :], fc1_bias).then_inc(columns_loaded, 16)
            pool.dma_start(s1_c[:, :, :], fc1_scales).then_inc(columns_loaded, 16)
            pool.dma_start(gamma_c[:, :], ln_gamma).then_inc(columns_loaded, 16)
            pool.dma_start(beta_c[:, :], ln_beta).then_inc(columns_loaded, 16)
            pool.memset(ident[:, :], 0.0).then_inc(pool_step, 1)
            pool.wait_ge(pool_step, 1)
            pool.affine_select(out=ident[:, :], in_=ident[:, :], compare_op=ALU.not_equal, fill=1.0,
                               base=0, pattern=[[-1, P]], channel_multiplier=1).then_inc(pool_step, 1)
            pool.memset(ones_row[:, :], 1.0).then_inc(pool_step, 1)

            def seed_gate(s):
                after(pool, xn_ready, s + 1)
                pool.tensor_tensor(gate[:, bass.ds(s * (GPS * EMB), GPS * EMB)].rearrange("p (g e) -> p g e", g=GPS),
                                   xn[:, :, :], b2_b[:, :].unsqueeze(1).to_broadcast([P, GPS, EMB]),
                                   ALU.add).then_inc(gate_seeded, 1)

            def first_phase(s, odd, first, last):
                after(pool, q_tile_ready, s + 1)
                after(pool, norm2_ready, s)
                pool.tensor_tensor(q_sq[:, :], q_tile[:, :, :].rearrange("p g e -> p (g e)"),
                                   q_tile[:, :, :].rearrange("p g e -> p (g e)"), ALU.mult).then_inc(q_sq_ready, 1)
                if first:
                    pool.wait_ge(w1_ready, 1)
                    pool.wait_ge(w2_ready, 1)
                pool.tensor_copy(q_rows[:, bass.ds(s * (GPS * EMB), GPS * EMB)],
                                 q_tile[:, :, :].rearrange("p g e -> p (g e)")).then_inc(q_rows_saved, 1)
                if not last:
                    seed_gate(s + 1)

            pool.wait_ge(w_step, 2)
            pool.tensor_tensor(w1_lo[:, :, :].rearrange("p k n -> p (k n)"), st1f,
                               w1_hi[:, :, :].rearrange("p k n -> p (k n)").bitcast(fp32), ALU.subtract)\
                .then_inc(w1_ready, 1)
            pool.wait_ge(b2_halved, 1)
            seed_gate(0)
            pool.wait_ge(w_step, 4)
            pool.wait_ge(w2_loaded, 16 * (1 + FC))
            pool.tensor_tensor(w2[:, :, :].rearrange("p k n -> p (k n)"), w2[:, :, :].rearrange("p k n -> p (k n)"),
                               st2s, ALU.mult).then_inc(w2_ready, 1)
            pool.memset(keys[0][:, :].bitcast(fp32), 0.0)
            pool.memset(queries[0][:, :].bitcast(fp32), 0.0)
            pool.memset(nmax[:, :], 0.0).then_inc(pool_step, 1)
            pool.wait_ge(pool_step, 4)
            pool.memset(keys[0][64:66, :].bitcast(fp32), 1.0).then_inc(consts_ready, 1)
            pool.wait_ge(consts_ready, 1)
            all_sets(pool, first_phase)

            def build_values(g, b):
                after(pool, pv_done, (g - (NB - 1)) * CH)
                pool.tensor_copy(values[b][:, :, 0:HD].rearrange("p (h c) d -> p h c d", h=EH),
                                 q_rows[:, bass.ds(g * EMB, EMB)].rearrange("p (h d c) -> p h c d", h=EH, d=HD))\
                    .then_inc(values_ready, 1)

            def finish(g, b, n):
                pool.wait_ge(s_ready, n)
                after(pool, stored[b], (g - b) * 8)
                pool.tensor_tensor(res[b], s_sb[b], gate[:, bass.ds(g * EMB, EMB)], ALU.mult).then_inc(gated, 1)
                pool.wait_ge(gated, n + 1)
                pool.wait_ge(x_reloaded[b], (g - b) * 8 + 16)
                pool.tensor_tensor(res[b], res[b], x_re[b], ALU.add).then_inc(res_ready, 1)

            pool.wait_ge(y_ready, SETS * FC)
            pool.wait_ge(fc2_in_psum, SETS - 1)
            pool.wait_ge(q_rows_saved, SETS)
            pool.wait_ge(gate_seeded, SETS)
            for b in range(1, NB):
                pool.memset(keys[b][:, :].bitcast(fp32), 0.0)
                last = pool.memset(queries[b][:, :].bitcast(fp32), 0.0)
            for b in range(NB):
                last = pool.memset(values[b][:, :, :], 0.0)
            last.then_inc(late_consts, 1)
            pool.wait_ge(late_consts, 1)
            for b in range(NB):
                last = pool.memset(values[b][:, :, HD:HD + 1], 1.0)
            last.then_inc(pool_step, 1)
            pool.wait_ge(pool_step, 5)
            for b in range(1, NB):
                last = pool.memset(keys[b][64:66, :].bitcast(fp32), 1.0)
            last.then_inc(late_consts, 1)
            pool.wait_ge(late_consts, 2)
            pool.wait_ge(hn_ready, SETS)
            pool.wait_ge(q_rows_saved, SETS)
            build_values(0, 0)
            build_values(1, 1)
            pool.wait_ge(gate_ready, SETS)
            pool.sem_inc(gated, 1)

            def steady(g, u, first, last):
                if not last:
                    if not (isinstance(g, int) and g + 2 >= GROUPS):
                        build_values(g + 2, (u + 2) % NB)
                if not first:
                    finish(g - 1, (u + 1) % 2, g)

            for g in range(3):
                steady(g, g % 6, g == 0, False)
            with pool.Fori(0, (GROUPS - 2) // 6 - 1) as i:
                for u in range(6):
                    steady(i * 6 + (u + 3), (u + 3) % 6, False, False)
            for g in range(GROUPS - 5, GROUPS):
                steady(g, g % 6, False, False)
            finish(GROUPS - 1, (GROUPS - 1) % 2, GROUPS)

        @block.scalar
        def _(act):
            def turn_xn(s):
                act.wait_ge(xnT_in_psum, s + 1)
                act.activation(xnT[:, :], PA[:, :], ACT.Copy).then_inc(xnT_ready, 1)

            def round_h(s):
                act.wait_ge(hT_ready, s + 1)
                after(act, fc1_in_psum, s * FC)
                act.activation(hT_hi[:, :], hT[:, :], ACT.Copy).then_inc(hT_hi_ready, 1)

            def silu_gate(s):
                act.wait_ge(z_added, s + 1)
                part = gate[:, bass.ds(s * (GPS * EMB), GPS * EMB)]
                act.activation(part, part, ACT.Silu).then_inc(gate_ready, 1)

            def first_phase(s, odd, first, last):
                for f in range(FC):
                    act.wait_ge(fc1_in_psum, s * FC + (f + 1))
                    act.activation(y_part[:, :], fc1_ps[f][:, 0:SR], ACT.Identity, bias=b1_c[:, f:f + 1],
                                   scale=s1_c[:, f, 0:1]).then_inc(y_part_ready, 1)
                    if f == 0:
                        act.wait_ge(qT_in_psum, s + 1)
                        after(act, qT_saved, s * (2 * EH * 16))
                        act.activation(qT_hi[:, :, :, :].rearrange("p h g r -> p (h g r)"), PB[:, :], ACT.Copy)\
                            .then_inc(qT_hi_ready, 1)
                    if f == 6 and not last:
                        turn_xn(s + 1)
                    act.wait_ge(y_sum_ready, s * FC + (f + 1))
                    if f == 0 and not first:
                        after(act, fc2_in_psum, s - 1 if isinstance(s, int) else 0)
                    act.activation(yT[odd][f], y_sum[:, :], ACT.Silu).then_inc(y_ready, 1)
                if not last:
                    round_h(s + 1)
                if not first:
                    silu_gate(s - 1)

            flat_hi, flat_lo = (w[:, :, :].rearrange("p k n -> p (k n)") for w in (w1_hi, w1_lo))
            act.wait_ge(w1_loaded, 16)
            act.activation(st1f, st1, ACT.Copy, bias=-128.0).then_inc(w_step, 1)
            act.wait_ge(w_step, 1)
            act.activation(flat_hi, st1f, ACT.Copy).then_inc(w_step, 1)
            turn_xn(0)
            act.wait_ge(w1_ready, 1)
            act.activation(w2[:, :, :].rearrange("p k n -> p (k n)"), flat_lo.bitcast(fp32), ACT.Square,
                           accum_out=low_max[:, :]).then_inc(w_step, 1)
            round_h(0)
            act.wait_ge(w2_loaded, 16 * (1 + FC))
            act.wait_ge(w_step, 3)
            act.activation(w2[:, :, :].rearrange("p k n -> p (k n)"), st2, ACT.Copy, bias=-128.0).then_inc(w_step, 1)
            act.wait_ge(small_loaded, 48)
            act.wait_ge(columns_loaded, 64)
            all_sets(act, first_phase)
            silu_gate(SETS - 1)

            def attention(g, u, first, last):
                for c in range(CH):
                    for h in range(2):
                        half = (u * CH + c) * 2 + h
                        act.wait_ge(scored, g * (2 * CH) + (2 * c + h + 1))
                        if h == 0:
                            after(act, pv_done, g * CH + (c - (NB - 1)))
                        at = ((u * CH + c) % NB) * QS * QT + h * 2 * QT
                        act.activation(ring[:, at:at + 2 * QT], score_ps[half % NB][:, :], ACT.Exp,
                                       scale=SCALE).then_inc(exped, 1)

            act.wait_ge(fc2_in_psum, SETS)
            all_groups(act, attention)

        @block.vector
        def _(dve):
            def layer_norm(s):
                step = [0]

                def link(ins):
                    step[0] += 1
                    ins.then_inc(ln_step, 1)
                    dve.wait_ge(ln_step, s * LN_STEPS + step[0])

                dve.wait_ge(x_loaded, s * 16 + 16)
                for n, (src, dst, done) in enumerate(((x_in, xn, xn_ready), (xn, hn, hn_ready))):
                    for g in range(GPS):
                        last = dve.bn_stats(stats[:, g, :], src[:, g, :])
                    link(last)
                    dve.tensor_tensor(mu[:, :], stats[:, :, 1], stats[:, :, 4], ALU.add)
                    dve.tensor_tensor(nt[:, :], stats[:, :, 1], stats[:, :, 4], ALU.subtract)
                    link(dve.tensor_tensor(ve[:, :], stats[:, :, 2], stats[:, :, 5], ALU.add))
                    dve.tensor_scalar(mu[:, :], mu[:, :], 0.5, None, ALU.mult)
                    dve.scalar_tensor_tensor(out=nt[:, :], in0=nt[:, :], scalar=0.25, in1=nt[:, :],
                                             op0=ALU.mult, op1=ALU.mult)
                    link(dve.tensor_scalar(ve[:, :], ve[:, :], 1.0 / EMB, EPS, ALU.mult, ALU.add))
                    link(dve.tensor_tensor(ve[:, :], ve[:, :], nt[:, :], ALU.add))
                    yield
                    link(dve.tensor_scalar(rs[:, :].bitcast(i32), ve[:, :].bitcast(i32), 1, None,
                                           ALU.logical_shift_right))
                    link(dve.tensor_scalar(rs[:, :].bitcast(i32), rs[:, :].bitcast(i32), -1.0, float(0x5F3759DF),
                                           ALU.mult, ALU.add))
                    for _ in range(3):
                        link(dve.scalar_tensor_tensor(out=nt[:, :], in0=rs[:, :], scalar=-0.5, in1=rs[:, :],
                                                      op0=ALU.mult, op1=ALU.mult))
                        link(dve.tensor_tensor(nt[:, :], nt[:, :], ve[:, :], ALU.mult))
                        link(dve.scalar_tensor_tensor(out=rs[:, :], in0=nt[:, :], scalar=1.5, in1=rs[:, :],
                                                      op0=ALU.add, op1=ALU.mult))
                    yield
                    if n == 0:
                        after(dve, xnT_in_psum, s)
                        after(dve, hT_in_psum, s)
                        after(dve, gate_seeded, s)
                    for g in range(GPS):
                        last = dve.tensor_scalar(dst[:, g, :], src[:, g, :], mu[:, g:g + 1], rs[:, g:g + 1],
                                                 ALU.subtract, ALU.mult)
                    last.then_inc(done, 1)
                    if n == 0:
                        dve.wait_ge(xn_ready, s + 1)
                    yield
                assert step[0] == LN_STEPS

            def turn_h(s):
                dve.wait_ge(hT_in_psum, s + 1)
                for h in range(EH):
                    last = dve.tensor_scalar(hT[:, h * SR:(h + 1) * SR], PB[:, h * SR:(h + 1) * SR],
                                             gamma_c[:, h:h + 1], beta_c[:, h:h + 1], ALU.mult, ALU.add)
                last.then_inc(hT_ready, 1)

            def split_h(s):
                dve.wait_ge(hT_hi_ready, s + 1)
                dve.wait_ge(hT_ready, s + 1)
                dve.tensor_tensor(hT_lo[:, :], hT[:, :], hT_hi[:, :].bitcast(fp32), ALU.subtract)\
                    .then_inc(hT_lo_ready, 1)

            def hidden(s, f):
                dve.wait_ge(y_part_ready, s * FC + (f + 1))
                dve.scalar_tensor_tensor(out=y_sum[:, :], in0=fc1_ps[f][:, SR:2 * SR], scalar=s1_c[:, f, 1:2],
                                         in1=y_part[:, :], op0=ALU.mult, op1=ALU.add).then_inc(y_sum_ready, 1)

            def add_z(s):
                dve.wait_ge(fc2_in_psum, s + 1)
                dve.wait_ge(gate_seeded, s + 1)
                part = gate[:, bass.ds(s * (GPS * EMB), GPS * EMB)]
                dve.scalar_tensor_tensor(out=part, in0=PD[:, :], scalar=0.5, in1=part, op0=ALU.mult, op1=ALU.add)\
                    .then_inc(z_added, 1)

            def squared_norms(s):
                dve.wait_ge(q_sq_ready, s + 1)
                dve.tensor_reduce(norm2[:, bass.ds(s * (GPS * CH), GPS * CH)].rearrange("p (t c) -> p t c", c=CH // EH),
                                  q_sq[:, :].rearrange("p (t d c) -> p t c d", d=HD, c=CH // EH), AX.X, ALU.add)\
                    .then_inc(norm2_ready, 1)

            def find_shift(part):
                if part == 0:
                    dve.wait_ge(norm2_ready, SETS)
                    dve.wait_ge(pool_step, 4)
                    dve.tensor_reduce(nmax[:, :], norm2[:, :], AX.X, ALU.max).then_inc(shift_step, 1)
                elif part == 1:
                    dve.wait_ge(shift_pe, 1)
                    dve.tensor_reduce(top[:, :], PA[0:1, 0:P], AX.X, ALU.max).then_inc(shift_step, 1)
                    dve.wait_ge(shift_step, 2)
                    dve.tensor_scalar(flag[:, :], top[:, :], COMMON_MAX_LIMIT / SCALE, None, ALU.is_gt).then_inc(flag_ready, 1)
                elif part == 2:
                    dve.wait_ge(shift_pe, 2)
                    dve.tensor_copy(nmax[:, :], PA[:, QT:QT + 1]).then_inc(shift_step, 1)
                    dve.wait_ge(shift_step, 3)
                    dve.tensor_scalar(shift[:, :], norm2[:, :], nmax[:, 0:1], None, ALU.max).then_inc(shift_step, 1)
                    dve.wait_ge(flag_ready, 1)
                    wide = dve.value_load(flag[0:1, 0:1])
                    with dve.If(wide):
                        dve.wait_ge(norm2_ready, SETS)
                        dve.wait_ge(shift_step, 4)
                        dve.memset(q_sq[:, :], 0.0).then_inc(gen_reduced, 1)
                        dve.wait_ge(gen_reduced, 1)
                        with dve.Fori(0, GROUPS) as g:
                            for c in range(CH):
                                for h in range(2):
                                    dve.wait_ge(gen_scored, g * (2 * CH) + (2 * c + h + 1))
                                    dve.tensor_reduce(q_sq[:, bass.ds(g * (2 * CH) + (2 * c + h), 1)],
                                                      PA[:, :], AX.X, ALU.max).then_inc(gen_reduced, 1)
                        dve.wait_ge(gen_reduced, GROUPS * 2 * CH + 1)
                        dve.tensor_reduce(shift[:, :], q_sq[:, :].rearrange("p (t h) -> p t h", h=2), AX.X, ALU.max)\
                            .then_inc(shift_step, 1)
                        dve.wait_ge(shift_step, 5)
                    dve.wait_ge(shift_step, 4)
                    dve.tensor_copy(nmax[:, :], shift[:, 0:1]).then_inc(shift_ready, 1)
                else:
                    dve.wait_ge(shift_pe, 3)
                    dve.wait_ge(qT_saved, SETS * 2 * EH * 16)
                    dve.tensor_scalar(neg, PA[:, 0:QT], -1.0, None, ALU.mult).then_inc(neg_ready, 1)
                    dve.tensor_scalar(neg_hi, PA[:, 0:QT], -1.0, None, ALU.mult).then_inc(shift_ready, 1)
                    dve.wait_ge(neg_ready, 1)
                    dve.wait_ge(shift_ready, 2)
                    dve.tensor_tensor(neg_lo, neg, neg_hi.bitcast(fp32), ALU.subtract).then_inc(neg_ready, 1)

            def first_phase(s, odd, first, last):
                norm = None if last else layer_norm(s + 1)
                if first:
                    dve.wait_ge(low_in_psum, 1)
                    dve.tensor_reduce(low_top[:, :], PC[0:1, 0:P], AX.X, ALU.max).then_inc(low_top_ready, 1)
                    dve.wait_ge(low_top_ready, 1)
                    dve.tensor_scalar(w_flag[:, :], low_top[:, :], 0.0, None, ALU.is_gt).then_inc(w_flag_ready, 1)
                dve.wait_ge(q_in_psum, s + 1)
                after(dve, q_sq_ready, s)
                after(dve, q_rows_saved, s)
                after(dve, qT_in_psum, s)
                dve.tensor_tensor(q_tile[:, :, :], PA[:, :].rearrange("p (g e) -> p g e", g=GPS),
                                  bq_b[:, :].unsqueeze(1).to_broadcast([P, GPS, EMB]), ALU.add)\
                    .then_inc(q_tile_ready, 1)
                hidden(s, 0)
                dve.wait_ge(qT_hi_ready, s + 1)
                after(dve, qT_saved, s * (2 * EH * 16))
                dve.tensor_tensor(qT_lo[:, :, :, :].rearrange("p h g r -> p (h g r)"), PB[:, :],
                                  qT_hi[:, :, :, :].rearrange("p h g r -> p (h g r)").bitcast(fp32),
                                  ALU.subtract).then_inc(qT_lo_ready, 1)
                for f in range(1, FC):
                    hidden(s, f)
                    if 1 <= f <= 6 and not last:
                        next(norm)
                    if last and f == 2:
                        squared_norms(s)
                        find_shift(0)
                    if last and 4 <= f <= 6:
                        find_shift(f - 3)
                if not last:
                    for _ in norm:
                        raise AssertionError("a seventh part")
                    turn_h(s + 1)
                if not first:
                    add_z(s - 1)
                if not last:
                    split_h(s + 1)
                    squared_norms(s)

            for _ in layer_norm(0):
                pass
            dve.wait_ge(small_loaded, 48)
            dve.wait_ge(columns_loaded, 64)
            dve.tensor_scalar(b2_b[:, :], b2_b[:, :], 0.5, None, ALU.mult).then_inc(b2_halved, 1)
            turn_h(0)
            split_h(0)
            all_sets(dve, first_phase)

            add_z(SETS - 1)

            def normalise(g, b, n):
                dve.wait_ge(pv_done, n * CH)
                dve.tensor_copy(acc_sb, acc_ps[b]).then_inc(acc_copied, 1)
                dve.wait_ge(acc_turned, n)
                turned = acc_ps[b].rearrange("p (c q m) -> p c q m", q=QS, m=VW)
                dve.reciprocal(rden, turned[:, :, :, HD]).then_inc(rden_ready, 1)
                dve.wait_ge(rden_ready, n)
                dve.tensor_tensor(attn[b].rearrange("p (q c d) -> p c q d", q=QS, d=HD), turned[:, :, :, 0:HD],
                                  rden.unsqueeze(3).to_broadcast([P, CH // QS, QS, HD]), ALU.mult)\
                    .then_inc(attn_ready, 1)

            def project(g, b, n):
                dve.wait_ge(attnT_in_psum, n)
                dve.tensor_copy(attnT.rearrange("p h n -> p (h n)"), acc_ps[b][:, 0:EH * P]).then_inc(attnT_ready, 1)
                dve.wait_ge(s_in_psum, n)
                dve.wait_ge(gated, n)
                dve.tensor_tensor(s_sb[b], acc_ps[b][:, 0:EMB], bu_b[:, :], ALU.add).then_inc(s_ready, 1)

            def attention(g, u, first, last):
                if not first:
                    normalise(g - 1, (u + 1) % 2, g)
                    project(g - 1, (u + 1) % 2, g)

            dve.wait_ge(wu_loaded, 32)
            dve.wait_ge(gate_seeded, SETS)
            all_groups(dve, attention)
            normalise(GROUPS - 1, (GROUPS - 1) % 2, GROUPS)
            project(GROUPS - 1, (GROUPS - 1) % 2, GROUPS)

        @block.tensor
        def _(pe):
            def turn_xn(s):
                pe.wait_ge(xn_ready, s + 1)
                after(pe, q_tile_ready, s)
                for h in range(EH):
                    for g in range(GPS):
                        mm = pe.transpose(PA[:, h * SR + g * P:h * SR + (g + 1) * P],
                                          xn[:, g, h * P:(h + 1) * P], ident[:, :])
                mm.then_inc(xnT_in_psum, 1)

            def turn_hn(s):
                pe.wait_ge(hn_ready, s + 1)
                after(pe, y_sum_ready, s * FC - 1)
                for h in range(EH):
                    for g in range(GPS):
                        mm = pe.transpose(PB[:, h * SR + g * P:h * SR + (g + 1) * P],
                                          hn[:, g, h * P:(h + 1) * P], ident[:, :])
                mm.then_inc(hT_in_psum, 1)

            def fc1(s, f, pieces):
                before = max([n for n in range(f) if fc1_ps[n] is fc1_ps[f]], default=-1)
                if before >= 0 or f == 0:
                    after(pe, y_sum_ready, s * FC + before + 1)
                else:
                    pe.wait_ge(qT_lo_ready, s + 1)
                for k in range(EH):
                    for n, (w, h) in enumerate(pieces):
                        mm = pe.matmul(fc1_ps[f][:, k * QT:(k + 1) * QT], w[:, k, f * P:(f + 1) * P],
                                       h[:, k * SR:(k + 1) * SR], start=(n == 0), stop=(n == len(pieces) - 1))
                mm.then_inc(fc1_in_psum, 1)

            def fc2(odd, half):
                g = half // 2
                for k in range(half % 2 * FC // 2, (half % 2 + 1) * FC // 2):
                    mm = pe.matmul(PD[:, g * FB:(g + 1) * FB], yT[odd][k][:, g * P:(g + 1) * P], w2[:, k, :],
                                   start=(k == 0), stop=(k == FC - 1))
                if half == 2 * GPS - 1:
                    mm.then_inc(fc2_in_psum, 1)

            def first_phase(s, odd, first, last):
                pe.wait_ge(xnT_ready, s + 1)
                for g in range(GPS):
                    for k in range(EH):
                        mm = pe.matmul(PA[:, g * FB:(g + 1) * FB], xnT[:, k * SR + g * P:k * SR + (g + 1) * P],
                                       wq_sb[:, k, :], start=(k == 0), stop=(k == EH - 1))
                mm.then_inc(q_in_psum, 1)
                pe.wait_ge(hT_lo_ready, s + 1)
                pe.wait_ge(hT_hi_ready, s + 1)
                if first:
                    pe.wait_ge(w_step, 3)
                    pe.transpose(PC[0:1, 0:P], low_max[:, :], ident[:, :]).then_inc(low_in_psum, 1)
                    pe.wait_ge(w_flag_ready, 1)
                    wide_w.append(pe.value_load(w_flag[0:1, 0:1]))
                with pe.If(wide_w[0]):
                    ffn(s, odd, first, last, [(w1_lo, hT_lo), (w1_lo, hT_hi), (w1_hi, hT_lo), (w1_hi, hT_hi)])
                with pe.Else():
                    ffn(s, odd, first, last, [(w1_hi, hT_lo), (w1_hi, hT_hi)])

            def ffn(s, odd, first, last, pieces):
                for f in range(FC):
                    if last and 4 <= f <= 6:
                        find_shift(f - 4)
                    fc1(s, f, pieces)
                    if f == 0:
                        pe.wait_ge(q_tile_ready, s + 1)
                        pe.wait_ge(hT_ready, s + 1)
                        for h in range(EH):
                            for g in range(GPS):
                                mm = pe.transpose(PB[:, h * SR + g * P:h * SR + (g + 1) * P],
                                                  q_tile[:, g, h * P:(h + 1) * P], ident[:, :])
                        mm.then_inc(qT_in_psum, 1)
                        after(pe, y_ready, s * FC)
                        if not first:
                            pe.wait_ge(w2_ready, 1)
                    if not last and f == 7:
                        turn_hn(s + 1)
                    if not first:
                        fc2(1 - odd, f)
                    if not last and f == 5:
                        turn_xn(s + 1)

            def find_shift(part):
                if part == 0:
                    pe.wait_ge(shift_step, 1)
                    pe.wait_ge(q_tile_ready, SETS)
                    pe.transpose(PA[0:1, 0:P], nmax[:, 0:1], ident[:, :]).then_inc(shift_pe, 1)
                elif part == 1:
                    pe.wait_ge(shift_step, 2)
                    pe.matmul(PA[:, QT:QT + 1], ones_row[0:1, :], top[0:1, 0:1], start=True, stop=True)\
                        .then_inc(shift_pe, 1)
                else:
                    pe.wait_ge(flag_ready, 1)
                    wide = pe.value_load(flag[0:1, 0:1])
                    with pe.If(wide):
                        pe.wait_ge(qT_lo_ready, SETS)
                        pe.wait_ge(shift_step, 4)
                        with pe.Fori(0, GROUPS) as g:
                            pe.wait_ge(gen_loaded, g * (GEN_DMAS * 16) + GEN_DMAS * 16)
                            for c in range(CH):
                                for h in range(2):
                                    pe.wait_ge(gen_reduced, g * (2 * CH) + (2 * c + h + 1))
                                    for j in range(2):
                                        mm = pe.matmul(PA[:, j * QT:(j + 1) * QT], keys[0][:, c * P:(c + 1) * P],
                                                       queries[0][:, (2 * h + j) * QT:(2 * h + j + 1) * QT],
                                                       start=True, stop=True)
                                    mm.then_inc(gen_scored, 1)
                    pe.wait_ge(shift_ready, 1)
                    for b in range(4):
                        mm = pe.transpose(PA[:, b * P:(b + 1) * P], shift[:, b * P:(b + 1) * P], ident[:, :])
                    mm.then_inc(shift_pe, 1)

            wide_w = []
            pe.wait_ge(pool_step, 3)
            turn_xn(0)
            turn_hn(0)
            pe.wait_ge(small_loaded, 48)
            pe.wait_ge(columns_loaded, 64)
            all_sets(pe, first_phase)
            pe.wait_ge(y_ready, SETS * FC)
            pe.wait_ge(z_added, SETS - 1)
            for half in range(2 * GPS):
                fc2(1, half)

            def scores(g, u, c):
                if c == 0:
                    pe.wait_ge(stack_loaded[u % NB], stack_count(g, u % NB))
                for h in range(2):
                    half = (u * CH + c) * 2 + h
                    after(pe, exped, g * (2 * CH) + (2 * c + h - (NB - 1)))
                    for j in range(2):
                        q = 2 * h + j
                        mm = pe.matmul(score_ps[half % NB][:, j * QT:(j + 1) * QT], keys[u % NB][:, c * P:(c + 1) * P],
                                       queries[u % NB][:, q * QT:(q + 1) * QT], start=True, stop=True)
                    mm.then_inc(scored, 1)

            def stack_count(g, b):
                return (g - b) * (STACK_DMAS * 16 // NB) + STACK_DMAS * 16

            def weigh(g, u, c):
                if c == 0:
                    pe.wait_ge(values_ready, g + 1)
                pe.wait_ge(exped, g * (2 * CH) + (2 * c + 2))
                at = ((u * CH + c) % NB) * QS * QT
                for q in range(QS):
                    mm = pe.matmul(acc_ps[u % 2][q * VW:(q + 1) * VW, :], values[u % NB][:, c, :],
                                   ring[:, at + q * QT:at + (q + 1) * QT], start=(c == 0), stop=(c == CH - 1),
                                   skip_group_check=True)
                mm.then_inc(pv_done, 1)

            def turn_acc(b, n):
                pe.wait_ge(acc_copied, n)
                for c in range(QT // P):
                    mm = pe.transpose(acc_ps[b][:, c * P:(c + 1) * P], acc_sb[:, c * P:(c + 1) * P], ident[:, :])
                mm.then_inc(acc_turned, 1)

            def turn_attn(b, n):
                pe.wait_ge(attn_ready, n)
                for h in range(EH):
                    mm = pe.transpose(acc_ps[b][:, h * P:(h + 1) * P], attn[b][:, h * P:(h + 1) * P], ident[:, :])
                mm.then_inc(attnT_in_psum, 1)

            def project(b, n):
                pe.wait_ge(attnT_ready, n)
                for h in range(EH):
                    mm = pe.matmul(acc_ps[b][:, 0:EMB], attnT[:, h, :], wu_sb[:, h, :], start=(h == 0), stop=(h == EH - 1))
                mm.then_inc(s_in_psum, 1)

            def attention(g, u, first, last):
                for c in range(CH):
                    if c + 1 < CH:
                        scores(g, u, c + 1)
                    elif not last:
                        scores(g + 1, (u + 1) % 6, 0)
                    weigh(g, u, c)
                    if not first:
                        b = (u + 1) % 2
                        if c == 1:
                            turn_acc(b, g)
                        if c == 3:
                            turn_attn(b, g)
                        if c == 5:
                            project(b, g)
                        if c == CH - 1:
                            pe.wait_ge(s_ready, g)

            pe.wait_ge(shift_pe, 3)
            pe.wait_ge(y_sum_ready, SETS * FC)
            pe.wait_ge(z_added, SETS)
            pe.wait_ge(neg_ready, 2)
            pe.wait_ge(qT_lo_ready, SETS)
            pe.wait_ge(wu_loaded, 32)
            scores(0, 0, 0)
            all_groups(pe, attention)
            turn_acc((GROUPS - 1) % 2, GROUPS)
            turn_attn((GROUPS - 1) % 2, GROUPS)
            project((GROUPS - 1) % 2, GROUPS)


_INS = ["x", "wqT", "bq", "wuT", "bu", "ln_gamma", "ln_beta", "fc1_q", "fc1_scales", "fc1_bias",
        "fc2_q", "fc2_scales", "fc2_bias"]


def kernel(L0_attn_x, L0_attn_wq, L0_attn_bq, L0_attn_wu, L0_attn_bu, L0_ffn_ln_gamma, L0_ffn_ln_beta,
           L0_ffn_fc1_q, L0_ffn_fc1_scales, L0_ffn_fc1_bias, L0_ffn_fc2_q, L0_ffn_fc2_scales, L0_ffn_fc2_bias):
    import numpy as np
    import concourse.bacc as bacc
    from concourse import mybir as mb
    from concourse.bass_utils import run_bass_kernel_spmd as run

    def columns(a):
        return np.asarray(a).reshape(-1, 128).T

    def by_place(a):
        a = np.asarray(a)
        return a.reshape(a.shape[:-1] + (2, 8, 16)).swapaxes(-1, -2).reshape(a.shape)

    shape = L0_attn_x.shape
    rows = shape[0] * shape[1]
    arrays = [np.asarray(L0_attn_x).reshape(rows, shape[2]), by_place(np.asarray(L0_attn_wq).T), by_place(L0_attn_bq),
              np.asarray(L0_attn_wu).T, L0_attn_bu, columns(L0_ffn_ln_gamma), columns(L0_ffn_ln_beta), L0_ffn_fc1_q,
              np.asarray(L0_ffn_fc1_scales).reshape(2, -1, 128).T, columns(L0_ffn_fc1_bias), L0_ffn_fc2_q, L0_ffn_fc2_scales, L0_ffn_fc2_bias]
    nc = bacc.Bacc("TRN2", target_bir_lowering=False, num_devices=1)
    ins, args = {}, []
    for name, a in zip(_INS, arrays):
        a = np.ascontiguousarray(a)
        ins[f"in_{name}"] = a
        args.append(nc.dram_tensor(f"in_{name}", a.shape, mb.dt.from_np(a.dtype), kind="ExternalInput").ap())
    args.append(nc.dram_tensor("out_rows", (rows, shape[2]), mb.dt.float32, kind="ExternalOutput").ap())
    groups = rows // 128
    args.append(nc.dram_tensor("qT_scratch", (groups, 2, 2, 16, 1024), mb.dt.float32, kind="Internal").ap())
    args.append(nc.dram_tensor("shift_scratch", (2, groups * 16, 128), mb.dt.float32, kind="Internal").ap())
    attention_times_ffn_gate(nc, *args)
    r = run(nc, [ins], core_ids=[0])
    return r.results[0]["out_rows"].reshape(shape)
```

```python
import concourse.bass as bass
from concourse import mybir
from contextlib import ExitStack

COMMON_MAX_LIMIT = 60.0


def attention_times_ffn_gate(
    nc: bass.Bass,
    x: bass.AP,
    wqT: bass.AP,
    bq: bass.AP,
    wuT: bass.AP,
    bu: bass.AP,
    ln_gamma: bass.AP,
    ln_beta: bass.AP,
    fc1_q: bass.AP,
    fc1_scales: bass.AP,
    fc1_bias: bass.AP,
    fc2_q: bass.AP,
    fc2_scales: bass.AP,
    fc2_bias: bass.AP,
    out: bass.AP,
    qT_scratch: bass.AP,
    shift_scratch: bass.AP,
):
    fp32 = mybir.dt.float32
    f32r = mybir.dt.float32r
    i32 = mybir.dt.int32
    ALU = mybir.AluOpType
    ACT = mybir.ActivationFunctionType
    AX = mybir.AxisListType

    P = 128
    ROWS, EMB = x.shape
    HD = 16
    CH = EMB // HD
    GROUPS = ROWS // P
    TOK = P * CH
    GPS = 4
    SETS = GROUPS // GPS
    SR = GPS * P
    EH = EMB // P
    F = fc1_q.shape[1]
    FC = F // P
    FB = EMB
    EPS = 1e-5
    SCALE = float(EMB) ** -0.5
    LN_STEPS = 30

    NB = 3
    QT = 512
    QS = TOK // QT
    VW = 32
    STACK_DMAS = 6
    ROWMAX_DMAS = 5

    x_set = x.rearrange("(s g r) e -> s r g e", g=GPS, r=P)
    x_grp = x.rearrange("(g r) e -> g r e", r=P)
    out_grp = out.rearrange("(g r) e -> g r e", r=P)
    qT_w = qT_scratch.rearrange("(s g) h p d (c r) -> s h p (d c) g r", g=GPS, r=P)
    qT_r = qT_scratch.rearrange("g h p d n -> g (p d) h n")
    shift_w = shift_scratch.rearrange("p (b k) r -> p k b r", k=P)
    shift_r = shift_scratch.rearrange("p (g c) r -> g p (c r)", c=CH)

    ctx = ExitStack()
    with ctx:
        def sb(name, shape, dt=fp32):
            return ctx.enter_context(nc.sbuf_tensor(name, shape, dt))

        def sem(name):
            return ctx.enter_context(nc.semaphore(name))

        q_rows = sb("q_rows", [P, GROUPS * EMB])
        gate = sb("gate", [P, GROUPS * EMB])
        ring = sb("ring", [P, NB * QS * QT])
        keys = [sb("keys0", [P, TOK], f32r)]
        queries = [sb("queries0", [P, TOK], f32r)]
        with ExitStack() as ffn:
            w1_hi = ffn.enter_context(nc.sbuf_tensor("w1_hi", [P, EH, F], f32r))
            w1_lo = ffn.enter_context(nc.sbuf_tensor("w1_lo", [P, EH, F], f32r))
            hT_hi = ffn.enter_context(nc.sbuf_tensor("hT_hi", [P, EH * SR], f32r))
            hT_lo = ffn.enter_context(nc.sbuf_tensor("hT_lo", [P, EH * SR], f32r))
            y_more = ffn.enter_context(nc.sbuf_tensor("y_more", [P, 4, SR], fp32))
        keys += [sb(f"keys{b}", [P, TOK], f32r) for b in range(1, NB)]
        queries += [sb(f"queries{b}", [P, TOK], f32r) for b in range(1, NB)]
        with ExitStack() as ffn:
            y_pre = [ffn.enter_context(nc.sbuf_tensor(f"y_pre{i}", [P, SR], fp32)) for i in range(2)]
        values = [sb(f"values{b}", [P, CH, VW]) for b in range(NB)]
        w2 = sb("w2", [P, FC, EMB])
        wq_sb = sb("wq_sb", [P, EH, EMB])
        wu_sb = sb("wu_sb", [P, EH, EMB])
        bq_b = sb("bq_b", [P, EMB])
        bu_b = sb("bu_b", [P, EMB])
        b2_b = sb("b2_b", [P, EMB])
        b1_c = sb("b1_c", [P, FC])
        s1_c = sb("s1_c", [P, FC, EH])
        w1_low_sq = sb("w1_low_sq", [P, 1])
        w1_low_top = sb("w1_low_top", [1, 1])
        w1_wide = sb("w1_wide", [1, 1], i32)
        gamma_c = sb("gamma_c", [P, EH])
        beta_c = sb("beta_c", [P, EH])
        ident = sb("ident", [P, P])
        ones_row = sb("ones_row", [1, P])
        x_in = sb("x_in", [P, GPS, EMB])
        xn = sb("xn", [P, GPS, EMB])
        hn = sb("hn", [P, GPS, EMB])
        xnT = sb("xnT", [P, EH * SR])
        hT = sb("hT", [P, EH * SR])
        q_tile = sb("q_tile", [P, GPS, EMB])
        q_sq = sb("q_sq", [P, GPS * EMB])
        qT_hi = sb("qT_hi", [P, EH, GPS, P], f32r)
        qT_lo = sb("qT_lo", [P, EH, GPS, P], f32r)
        stats = sb("stats", [P, GPS, 6])
        ln_mean = sb("ln_mean", [P, GPS])
        ln_var = sb("ln_var", [P, GPS])
        ln_rstd = sb("ln_rstd", [P, GPS])
        ln_tmp = sb("ln_tmp", [P, GPS])
        norm2 = sb("norm2", [P, GROUPS * CH])
        shift = sb("shift", [P, GROUPS * CH])
        norm_max = sb("norm_max", [P, 1])
        norm_top = sb("norm_top", [1, 1])
        scores_wide = sb("scores_wide", [1, 1], i32)

        y_tiles = [y_more[:, f, :] for f in range(4)] + [ring[:, f * SR:(f + 1) * SR] for f in range(2 * FC - 4)]
        yT = [y_tiles[:FC], y_tiles[FC:]]
        w1_int = q_rows[:, 0:EH * F].bitcast(i32)
        w1_float = q_rows[:, EH * F:2 * EH * F]
        w2_int = q_rows[:, 2 * EH * F:3 * EH * F].bitcast(i32)
        w2_scales = q_rows[:, 3 * EH * F:4 * EH * F]
        acc_sb = xnT[:, 0:QT]
        x_re = [x_in[:, 0, :], x_in[:, 1, :]]
        attn = [x_in[:, 2, :], x_in[:, 3, :]]
        attnT = hT[:, 0:EH * P].rearrange("p (h n) -> p h n", h=EH)
        s_sb = [xn[:, 0, :], xn[:, 1, :]]
        res = [xn[:, 2, :], xn[:, 3, :]]
        rden = hn[:, 0, 0:CH].rearrange("p (c q) -> p c q", c=CH // QS)
        neg = hn[:, 2:4, :].rearrange("p a b -> p (a b)")
        neg_hi = qT_hi[:, 0, :, :].rearrange("p a b -> p (a b)")
        neg_lo = qT_lo[:, 0, :, :].rearrange("p a b -> p (a b)")

        PA, PB, PC, PD = [ctx.enter_context(nc.psum_tensor(f"pair{i}", [P, 2 * QT], fp32)) for i in range(4)]
        score_ps = [PA, PB, PC]
        fc1_ps = [PC, PC, PB, PC, PB, PC, PB, PC]
        acc_ps = [PD[:, 0:QT], PD[:, QT:2 * QT]]

        x_loaded = sem("x_loaded")
        small_loaded = sem("small_loaded")
        columns_loaded = sem("columns_loaded")
        w1_loaded = sem("w1_loaded")
        w2_loaded = sem("w2_loaded")
        wu_loaded = sem("wu_loaded")
        w1_ready = sem("w1_ready")
        w2_ready = sem("w2_ready")
        b2_halved = sem("b2_halved")
        consts_ready = sem("consts_ready")
        pool_step = sem("pool_step")
        ln_step = sem("ln_step")
        xn_ready = sem("xn_ready")
        hn_ready = sem("hn_ready")
        gate_seeded = sem("gate_seeded")
        xnT_in_psum = sem("xnT_in_psum")
        hT_in_psum = sem("hT_in_psum")
        xnT_ready = sem("xnT_ready")
        hT_ready = sem("hT_ready")
        q_in_psum = sem("q_in_psum")
        q_tile_ready = sem("q_tile_ready")
        q_rows_saved = sem("q_rows_saved")
        q_sq_ready = sem("q_sq_ready")
        norm2_ready = sem("norm2_ready")
        qT_in_psum = sem("qT_in_psum")
        qT_hi_ready = sem("qT_hi_ready")
        qT_lo_ready = sem("qT_lo_ready")
        qT_saved = sem("qT_saved")
        fc1_in_psum = sem("fc1_in_psum")
        y_part_ready = sem("y_part_ready")
        y_sum_ready = sem("y_sum_ready")
        y_ready = sem("y_ready")
        hT_hi_ready = sem("hT_hi_ready")
        hT_lo_ready = sem("hT_lo_ready")
        w_step = sem("w_step")
        w1_low_top_ready = sem("w1_low_top_ready")
        w1_low_in_psum = sem("w1_low_in_psum")
        w1_wide_ready = sem("w1_wide_ready")
        late_consts = sem("late_consts")
        fc2_in_psum = sem("fc2_in_psum")
        z_added = sem("z_added")
        gate_ready = sem("gate_ready")
        shift_step = sem("shift_step")
        shift_pe = sem("shift_pe")
        scores_wide_ready = sem("scores_wide_ready")
        shift_ready = sem("shift_ready")
        neg_ready = sem("neg_ready")
        shift_saved = sem("shift_saved")
        rowmax_loaded = sem("rowmax_loaded")
        rowmax_scored = sem("rowmax_scored")
        rowmax_reduced = sem("rowmax_reduced")
        stack_loaded = [sem(f"stack_loaded{b}") for b in range(NB)]
        x_reloaded = [sem(f"x_reloaded{b}") for b in range(2)]
        values_ready = sem("values_ready")
        scored = sem("scored")
        exped = sem("exped")
        pv_done = sem("pv_done")
        acc_copied = sem("acc_copied")
        acc_turned = sem("acc_turned")
        rden_ready = sem("rden_ready")
        attn_ready = sem("attn_ready")
        attnT_in_psum = sem("attnT_in_psum")
        attnT_ready = sem("attnT_ready")
        s_in_psum = sem("s_in_psum")
        s_ready = sem("s_ready")
        gated = sem("gated")
        res_ready = sem("res_ready")
        stored = [sem(f"stored{b}") for b in range(2)]

        def after(eng, s, count):
            if not isinstance(count, int) or count > 0:
                eng.wait_ge(s, count)

        def all_sets(eng, step):
            step(0, 0, True, False)
            with eng.Fori(0, (SETS - 2) // 2) as i:
                step(i * 2 + 1, 1, False, False)
                step(i * 2 + 2, 0, False, False)
            step(SETS - 1, 1, False, True)

        def all_groups(eng, step):
            step(0, 0, True, False)
            with eng.Fori(0, (GROUPS - 2) // 6) as i:
                for u in range(6):
                    step(i * 6 + (u + 1), (u + 1) % 6, False, False)
            step(GROUPS - 1, (GROUPS - 1) % 6, False, True)

        block = ctx.enter_context(nc.Block())

        @block.sync
        def _(sp):
            def load_x(s):
                after(sp, xn_ready, s)
                sp.dma_start(x_in[:, :, :], x_set[s]).then_inc(x_loaded, 16)

            def save_qT(s):
                sp.wait_ge(qT_hi_ready, s + 1)
                for h in range(EH):
                    sp.dma_start(qT_w[s, h, 0], qT_hi[:, h, :, :].bitcast(fp32)).then_inc(qT_saved, 16)
                sp.wait_ge(qT_lo_ready, s + 1)
                for h in range(EH):
                    sp.dma_start(qT_w[s, h, 1], qT_lo[:, h, :, :].bitcast(fp32)).then_inc(qT_saved, 16)

            def load_stack(g, b, s_done):
                sp.dma_start(keys[b][0:32, :].bitcast(fp32).rearrange("p (h n) -> p h n", h=EH), qT_r[g]).then_inc(s_done, 16)
                sp.dma_start(keys[b][32:64, :].bitcast(fp32).rearrange("p (h n) -> p h n", h=EH), qT_r[g]).then_inc(s_done, 16)
                sp.dma_start(queries[b][0:32, :].bitcast(fp32).rearrange("p (h n) -> p h n", h=EH), qT_r[g]).then_inc(s_done, 16)
                sp.dma_start(queries[b][32:48, :].bitcast(fp32).rearrange("p (h n) -> p h n", h=EH), qT_r[g, 16:32]).then_inc(s_done, 16)
                sp.dma_start(queries[b][48:64, :].bitcast(fp32).rearrange("p (h n) -> p h n", h=EH), qT_r[g, 0:16]).then_inc(s_done, 16)

            def first_phase(s, odd, first, last):
                if not last:
                    load_x(s + 1)
                save_qT(s)

            load_x(0)
            sp.dma_start(w1_int.rearrange("p (k n) -> p k n", k=EH), fc1_q.rearrange("(k p) n -> p k n", p=P)).then_inc(w1_loaded, 16)
            sp.dma_start(bq_b[:, :], bq[None, :].to_broadcast([P, EMB])).then_inc(small_loaded, 16)
            sp.dma_start(b2_b[:, :], fc2_bias[None, :].to_broadcast([P, EMB])).then_inc(small_loaded, 16)
            sp.dma_start(wq_sb[:, :, :], wqT.rearrange("(k p) n -> p k n", p=P)).then_inc(small_loaded, 16)
            sp.dma_start(w2_int.rearrange("p (k n) -> p k n", k=FC), fc2_q.rearrange("(k p) n -> p k n", p=P)).then_inc(w2_loaded, 16)
            for k in range(FC):
                sp.dma_start(w2_scales[:, k * EMB:(k + 1) * EMB], fc2_scales[k:k + 1, :].to_broadcast([P, EMB])).then_inc(w2_loaded, 16)
            sp.dma_start(bu_b[:, :], bu[None, :].to_broadcast([P, EMB])).then_inc(wu_loaded, 16)
            sp.dma_start(wu_sb[:, :, :], wuT.rearrange("(k p) n -> p k n", p=P)).then_inc(wu_loaded, 16)
            all_sets(sp, first_phase)

            sp.wait_ge(qT_saved, SETS * 2 * EH * 16)
            sp.wait_ge(consts_ready, 1)
            sp.wait_ge(scores_wide_ready, 1)
            wide = sp.value_load(scores_wide[0:1, 0:1])
            with sp.If(wide):
                load_stack(0, 0, rowmax_loaded)
                with sp.Fori(1, GROUPS) as g:
                    sp.wait_ge(rowmax_scored, g * (2 * CH))
                    load_stack(g, 0, rowmax_loaded)
                sp.wait_ge(rowmax_scored, GROUPS * 2 * CH)

            load_stack(0, 0, stack_loaded[0])
            sp.wait_ge(neg_ready, 2)
            sp.dma_start(shift_w[0], neg_hi.bitcast(fp32).rearrange("p (b r) -> p b r", b=4)).then_inc(shift_saved, 16)
            sp.dma_start(shift_w[1], neg_lo.bitcast(fp32).rearrange("p (b r) -> p b r", b=4)).then_inc(shift_saved, 16)
            sp.wait_ge(shift_saved, 32)
            sp.dma_start(queries[0][64:66, :].bitcast(fp32), shift_r[0]).then_inc(stack_loaded[0], 16)
            sp.wait_ge(late_consts, 2)
            for g in range(1, NB):
                load_stack(g, g, stack_loaded[g])
                sp.dma_start(queries[g][64:66, :].bitcast(fp32), shift_r[g]).then_inc(stack_loaded[g], 16)
            sp.wait_ge(xn_ready, SETS)

            def attention(g, u, first, last):
                sp.dma_start(x_re[u % 2], x_grp[g]).then_inc(x_reloaded[u % 2], 16)
                if not last:
                    sp.wait_ge(scored, (g + 1) * (2 * CH))
                    load_stack(g + NB, u % NB, stack_loaded[u % NB])
                    sp.dma_start(queries[u % NB][64:66, :].bitcast(fp32), shift_r[g + NB]).then_inc(stack_loaded[u % NB], 16)
                if not first:
                    sp.wait_ge(res_ready, g)
                    sp.dma_start(out_grp[g - 1], res[(u + 1) % 2]).then_inc(stored[(u + 1) % 2], 16)

            def attention_all():
                attention(0, 0, True, False)
                with sp.Fori(0, (GROUPS - 2) // 6 - 1) as i:
                    for u in range(6):
                        attention(i * 6 + (u + 1), (u + 1) % 6, False, False)
                for g in range(GROUPS - 7, GROUPS):
                    attention(g, g % 6, False, g + NB >= GROUPS)

            attention_all()
            sp.wait_ge(res_ready, GROUPS)
            sp.dma_start(out_grp[GROUPS - 1], res[(GROUPS - 1) % 2]).then_inc(stored[(GROUPS - 1) % 2], 16)
            for b in range(2):
                sp.wait_ge(stored[b], 16 * GROUPS // 2)

        @block.gpsimd
        def _(pool):
            pool.dma_start(b1_c[:, :], fc1_bias).then_inc(columns_loaded, 16)
            pool.dma_start(s1_c[:, :, :], fc1_scales).then_inc(columns_loaded, 16)
            pool.dma_start(gamma_c[:, :], ln_gamma).then_inc(columns_loaded, 16)
            pool.dma_start(beta_c[:, :], ln_beta).then_inc(columns_loaded, 16)
            pool.memset(ident[:, :], 0.0).then_inc(pool_step, 1)
            pool.wait_ge(pool_step, 1)
            pool.affine_select(out=ident[:, :], in_=ident[:, :], compare_op=ALU.not_equal, fill=1.0,
                               base=0, pattern=[[-1, P]], channel_multiplier=1).then_inc(pool_step, 1)
            pool.memset(ones_row[:, :], 1.0).then_inc(pool_step, 1)

            def seed_gate(s):
                after(pool, xn_ready, s + 1)
                pool.tensor_tensor(gate[:, bass.ds(s * (GPS * EMB), GPS * EMB)].rearrange("p (g e) -> p g e", g=GPS),
                                   xn[:, :, :], b2_b[:, :].unsqueeze(1).to_broadcast([P, GPS, EMB]),
                                   ALU.add).then_inc(gate_seeded, 1)

            def first_phase(s, odd, first, last):
                after(pool, q_tile_ready, s + 1)
                after(pool, norm2_ready, s)
                pool.tensor_tensor(q_sq[:, :], q_tile[:, :, :].rearrange("p g e -> p (g e)"),
                                   q_tile[:, :, :].rearrange("p g e -> p (g e)"), ALU.mult).then_inc(q_sq_ready, 1)
                if first:
                    pool.wait_ge(w1_ready, 1)
                    pool.wait_ge(w2_ready, 1)
                pool.tensor_copy(q_rows[:, bass.ds(s * (GPS * EMB), GPS * EMB)],
                                 q_tile[:, :, :].rearrange("p g e -> p (g e)")).then_inc(q_rows_saved, 1)
                if not last:
                    seed_gate(s + 1)

            pool.wait_ge(w_step, 2)
            pool.tensor_tensor(w1_lo[:, :, :].rearrange("p k n -> p (k n)"), w1_float,
                               w1_hi[:, :, :].rearrange("p k n -> p (k n)").bitcast(fp32), ALU.subtract)\
                .then_inc(w1_ready, 1)
            pool.wait_ge(b2_halved, 1)
            seed_gate(0)
            pool.wait_ge(w_step, 4)
            pool.wait_ge(w2_loaded, 16 * (1 + FC))
            pool.tensor_tensor(w2[:, :, :].rearrange("p k n -> p (k n)"), w2[:, :, :].rearrange("p k n -> p (k n)"),
                               w2_scales, ALU.mult).then_inc(w2_ready, 1)
            pool.memset(keys[0][:, :].bitcast(fp32), 0.0)
            pool.memset(queries[0][:, :].bitcast(fp32), 0.0)
            pool.memset(norm_max[:, :], 0.0).then_inc(pool_step, 1)
            pool.wait_ge(pool_step, 4)
            pool.memset(keys[0][64:66, :].bitcast(fp32), 1.0).then_inc(consts_ready, 1)
            pool.wait_ge(consts_ready, 1)
            all_sets(pool, first_phase)

            def build_values(g, b):
                after(pool, pv_done, g - (NB - 1))
                pool.tensor_copy(values[b][:, :, 0:HD].rearrange("p (h c) d -> p h c d", h=EH),
                                 q_rows[:, bass.ds(g * EMB, EMB)].rearrange("p (h d c) -> p h c d", h=EH, d=HD))\
                    .then_inc(values_ready, 1)

            def finish(g, b, n):
                pool.wait_ge(s_ready, n)
                after(pool, stored[b], (g - b) * 8)
                pool.tensor_tensor(res[b], s_sb[b], gate[:, bass.ds(g * EMB, EMB)], ALU.mult).then_inc(gated, 1)
                pool.wait_ge(gated, n + 1)
                pool.wait_ge(x_reloaded[b], (g - b) * 8 + 16)
                pool.tensor_tensor(res[b], res[b], x_re[b], ALU.add).then_inc(res_ready, 1)

            pool.wait_ge(y_ready, SETS * FC)
            pool.wait_ge(fc2_in_psum, SETS - 1)
            pool.wait_ge(q_rows_saved, SETS)
            pool.wait_ge(gate_seeded, SETS)
            for b in range(1, NB):
                pool.memset(keys[b][:, :].bitcast(fp32), 0.0)
                last = pool.memset(queries[b][:, :].bitcast(fp32), 0.0)
            for b in range(NB):
                last = pool.memset(values[b][:, :, :], 0.0)
            last.then_inc(late_consts, 1)
            pool.wait_ge(late_consts, 1)
            for b in range(NB):
                last = pool.memset(values[b][:, :, HD:HD + 1], 1.0)
            last.then_inc(pool_step, 1)
            pool.wait_ge(pool_step, 5)
            for b in range(1, NB):
                last = pool.memset(keys[b][64:66, :].bitcast(fp32), 1.0)
            last.then_inc(late_consts, 1)
            pool.wait_ge(late_consts, 2)
            pool.wait_ge(hn_ready, SETS)
            pool.wait_ge(q_rows_saved, SETS)
            build_values(0, 0)
            build_values(1, 1)
            pool.wait_ge(gate_ready, SETS)
            pool.sem_inc(gated, 1)

            def steady(g, u, first, last):
                if not last:
                    if not (isinstance(g, int) and g + 2 >= GROUPS):
                        build_values(g + 2, (u + 2) % NB)
                if not first:
                    finish(g - 1, (u + 1) % 2, g)

            for g in range(3):
                steady(g, g % 6, g == 0, False)
            with pool.Fori(0, (GROUPS - 2) // 6 - 1) as i:
                for u in range(6):
                    steady(i * 6 + (u + 3), (u + 3) % 6, False, False)
            for g in range(GROUPS - 5, GROUPS):
                steady(g, g % 6, False, False)
            finish(GROUPS - 1, (GROUPS - 1) % 2, GROUPS)

        @block.scalar
        def _(act):
            def turn_xn(s):
                act.wait_ge(xnT_in_psum, s + 1)
                act.activation(xnT[:, :], PA[:, :], ACT.Copy).then_inc(xnT_ready, 1)

            def round_h(s):
                act.wait_ge(hT_ready, s + 1)
                after(act, fc1_in_psum, s * FC)
                act.activation(hT_hi[:, :], hT[:, :], ACT.Copy).then_inc(hT_hi_ready, 1)

            def silu_gate(s):
                act.wait_ge(z_added, s + 1)
                part = gate[:, bass.ds(s * (GPS * EMB), GPS * EMB)]
                act.activation(part, part, ACT.Silu).then_inc(gate_ready, 1)

            def silu_hidden(s, odd, f):
                act.wait_ge(y_sum_ready, s * FC + (f + 1))
                act.activation(yT[odd][f], y_pre[f % 2][:, :], ACT.Silu).then_inc(y_ready, 1)

            def first_phase(s, odd, first, last):
                for f in range(FC):
                    act.wait_ge(fc1_in_psum, s * FC + (f + 1))
                    after(act, y_ready, s * FC + (f - 1))
                    act.activation(y_pre[f % 2][:, :], fc1_ps[f][:, 0:SR], ACT.Identity, bias=b1_c[:, f:f + 1],
                                   scale=s1_c[:, f, 0:1]).then_inc(y_part_ready, 1)
                    if f == 0:
                        act.wait_ge(qT_in_psum, s + 1)
                        after(act, qT_saved, s * (2 * EH * 16))
                        act.activation(qT_hi[:, :, :, :].rearrange("p h g r -> p (h g r)"), PB[:, :], ACT.Copy)\
                            .then_inc(qT_hi_ready, 1)
                    if f == 6 and not last:
                        turn_xn(s + 1)
                    if f > 0:
                        silu_hidden(s, odd, f - 1)
                silu_hidden(s, odd, FC - 1)
                if not last:
                    round_h(s + 1)
                if not first:
                    silu_gate(s - 1)

            flat_hi, flat_lo = (w[:, :, :].rearrange("p k n -> p (k n)") for w in (w1_hi, w1_lo))
            act.wait_ge(w1_loaded, 16)
            act.activation(w1_float, w1_int, ACT.Copy, bias=-128.0).then_inc(w_step, 1)
            act.wait_ge(w_step, 1)
            act.activation(flat_hi, w1_float, ACT.Copy).then_inc(w_step, 1)
            turn_xn(0)
            act.wait_ge(w1_ready, 1)
            act.activation(w2[:, :, :].rearrange("p k n -> p (k n)"), flat_lo.bitcast(fp32), ACT.Square,
                           accum_out=w1_low_sq[:, :]).then_inc(w_step, 1)
            round_h(0)
            act.wait_ge(w2_loaded, 16 * (1 + FC))
            act.wait_ge(w_step, 3)
            act.activation(w2[:, :, :].rearrange("p k n -> p (k n)"), w2_int, ACT.Copy, bias=-128.0).then_inc(w_step, 1)
            act.wait_ge(small_loaded, 48)
            act.wait_ge(columns_loaded, 64)
            all_sets(act, first_phase)
            silu_gate(SETS - 1)

            def attention(g, u, first, last):
                for c in range(CH):
                    for h in range(2):
                        half = (u * CH + c) * 2 + h
                        act.wait_ge(scored, g * (2 * CH) + (2 * c + h + 1))
                        at = ((u * CH + c) % NB) * QS * QT + h * 2 * QT
                        act.activation(ring[:, at:at + 2 * QT], score_ps[half % NB][:, :], ACT.Exp,
                                       scale=SCALE).then_inc(exped, 1)

            act.wait_ge(fc2_in_psum, SETS)
            all_groups(act, attention)

        @block.vector
        def _(dve):
            def layer_norm(s):
                step = [0]

                def link(ins):
                    step[0] += 1
                    ins.then_inc(ln_step, 1)
                    dve.wait_ge(ln_step, s * LN_STEPS + step[0])

                dve.wait_ge(x_loaded, s * 16 + 16)
                for n, (src, dst, done) in enumerate(((x_in, xn, xn_ready), (xn, hn, hn_ready))):
                    for g in range(GPS):
                        last = dve.bn_stats(stats[:, g, :], src[:, g, :])
                    link(last)
                    dve.tensor_tensor(ln_mean[:, :], stats[:, :, 1], stats[:, :, 4], ALU.add)
                    dve.tensor_tensor(ln_tmp[:, :], stats[:, :, 1], stats[:, :, 4], ALU.subtract)
                    link(dve.tensor_tensor(ln_var[:, :], stats[:, :, 2], stats[:, :, 5], ALU.add))
                    dve.tensor_scalar(ln_mean[:, :], ln_mean[:, :], 0.5, None, ALU.mult)
                    dve.scalar_tensor_tensor(out=ln_tmp[:, :], in0=ln_tmp[:, :], scalar=0.25, in1=ln_tmp[:, :],
                                             op0=ALU.mult, op1=ALU.mult)
                    link(dve.tensor_scalar(ln_var[:, :], ln_var[:, :], 1.0 / EMB, EPS, ALU.mult, ALU.add))
                    link(dve.tensor_tensor(ln_var[:, :], ln_var[:, :], ln_tmp[:, :], ALU.add))
                    yield
                    link(dve.tensor_scalar(ln_rstd[:, :].bitcast(i32), ln_var[:, :].bitcast(i32), 1, None,
                                           ALU.logical_shift_right))
                    link(dve.tensor_scalar(ln_rstd[:, :].bitcast(i32), ln_rstd[:, :].bitcast(i32), -1.0, float(0x5F3759DF),
                                           ALU.mult, ALU.add))
                    for _ in range(3):
                        link(dve.scalar_tensor_tensor(out=ln_tmp[:, :], in0=ln_rstd[:, :], scalar=-0.5, in1=ln_rstd[:, :],
                                                      op0=ALU.mult, op1=ALU.mult))
                        link(dve.tensor_tensor(ln_tmp[:, :], ln_tmp[:, :], ln_var[:, :], ALU.mult))
                        link(dve.scalar_tensor_tensor(out=ln_rstd[:, :], in0=ln_tmp[:, :], scalar=1.5, in1=ln_rstd[:, :],
                                                      op0=ALU.add, op1=ALU.mult))
                    yield
                    if n == 0:
                        after(dve, xnT_in_psum, s)
                        after(dve, hT_in_psum, s)
                        after(dve, gate_seeded, s)
                    for g in range(GPS):
                        last = dve.tensor_scalar(dst[:, g, :], src[:, g, :], ln_mean[:, g:g + 1], ln_rstd[:, g:g + 1],
                                                 ALU.subtract, ALU.mult)
                    last.then_inc(done, 1)
                    if n == 0:
                        dve.wait_ge(xn_ready, s + 1)
                    yield
                assert step[0] == LN_STEPS

            def turn_h(s):
                dve.wait_ge(hT_in_psum, s + 1)
                for h in range(EH):
                    last = dve.tensor_scalar(hT[:, h * SR:(h + 1) * SR], PB[:, h * SR:(h + 1) * SR],
                                             gamma_c[:, h:h + 1], beta_c[:, h:h + 1], ALU.mult, ALU.add)
                last.then_inc(hT_ready, 1)

            def split_h(s):
                dve.wait_ge(hT_hi_ready, s + 1)
                dve.wait_ge(hT_ready, s + 1)
                dve.tensor_tensor(hT_lo[:, :], hT[:, :], hT_hi[:, :].bitcast(fp32), ALU.subtract)\
                    .then_inc(hT_lo_ready, 1)

            def hidden(s, f):
                dve.wait_ge(y_part_ready, s * FC + (f + 1))
                dve.scalar_tensor_tensor(out=y_pre[f % 2][:, :], in0=fc1_ps[f][:, SR:2 * SR], scalar=s1_c[:, f, 1:2],
                                         in1=y_pre[f % 2][:, :], op0=ALU.mult, op1=ALU.add).then_inc(y_sum_ready, 1)

            def add_z(s, z_ps):
                dve.wait_ge(fc2_in_psum, s + 1)
                dve.wait_ge(gate_seeded, s + 1)
                part = gate[:, bass.ds(s * (GPS * EMB), GPS * EMB)]
                dve.scalar_tensor_tensor(out=part, in0=z_ps[:, :], scalar=0.5, in1=part, op0=ALU.mult, op1=ALU.add)\
                    .then_inc(z_added, 1)

            def squared_norms(s):
                dve.wait_ge(q_sq_ready, s + 1)
                dve.tensor_reduce(norm2[:, bass.ds(s * (GPS * CH), GPS * CH)].rearrange("p (t c) -> p t c", c=CH // EH),
                                  q_sq[:, :].rearrange("p (t d c) -> p t c d", d=HD, c=CH // EH), AX.X, ALU.add)\
                    .then_inc(norm2_ready, 1)

            def find_shift(part):
                if part == 0:
                    dve.wait_ge(norm2_ready, SETS)
                    dve.wait_ge(pool_step, 4)
                    dve.tensor_reduce(norm_max[:, :], norm2[:, :], AX.X, ALU.max).then_inc(shift_step, 1)
                elif part == 1:
                    dve.wait_ge(shift_pe, 1)
                    dve.tensor_reduce(norm_top[:, :], PA[0:1, 0:P], AX.X, ALU.max).then_inc(shift_step, 1)
                    dve.wait_ge(shift_step, 2)
                    dve.tensor_scalar(scores_wide[:, :], norm_top[:, :], COMMON_MAX_LIMIT / SCALE, None, ALU.is_gt).then_inc(scores_wide_ready, 1)
                elif part == 2:
                    dve.wait_ge(shift_pe, 2)
                    dve.tensor_copy(norm_max[:, :], PA[:, QT:QT + 1]).then_inc(shift_step, 1)
                    dve.wait_ge(shift_step, 3)
                    dve.tensor_scalar(shift[:, :], norm2[:, :], norm_max[:, 0:1], None, ALU.max).then_inc(shift_step, 1)
                    dve.wait_ge(scores_wide_ready, 1)
                    wide = dve.value_load(scores_wide[0:1, 0:1])
                    with dve.If(wide):
                        dve.wait_ge(norm2_ready, SETS)
                        dve.wait_ge(shift_step, 4)
                        dve.memset(q_sq[:, :], 0.0).then_inc(rowmax_reduced, 1)
                        dve.wait_ge(rowmax_reduced, 1)
                        with dve.Fori(0, GROUPS) as g:
                            for c in range(CH):
                                for h in range(2):
                                    dve.wait_ge(rowmax_scored, g * (2 * CH) + (2 * c + h + 1))
                                    dve.tensor_reduce(q_sq[:, bass.ds(g * (2 * CH) + (2 * c + h), 1)],
                                                      PA[:, :], AX.X, ALU.max).then_inc(rowmax_reduced, 1)
                        dve.wait_ge(rowmax_reduced, GROUPS * 2 * CH + 1)
                        dve.tensor_reduce(shift[:, :], q_sq[:, :].rearrange("p (t h) -> p t h", h=2), AX.X, ALU.max)\
                            .then_inc(shift_step, 1)
                        dve.wait_ge(shift_step, 5)
                    dve.wait_ge(shift_step, 4)
                    dve.tensor_copy(norm_max[:, :], shift[:, 0:1]).then_inc(shift_ready, 1)
                else:
                    dve.wait_ge(shift_pe, 3)
                    dve.wait_ge(qT_saved, SETS * 2 * EH * 16)
                    dve.tensor_scalar(neg, PA[:, 0:QT], -1.0, None, ALU.mult).then_inc(neg_ready, 1)
                    dve.tensor_scalar(neg_hi, PA[:, 0:QT], -1.0, None, ALU.mult).then_inc(shift_ready, 1)
                    dve.wait_ge(neg_ready, 1)
                    dve.wait_ge(shift_ready, 2)
                    dve.tensor_tensor(neg_lo, neg, neg_hi.bitcast(fp32), ALU.subtract).then_inc(neg_ready, 1)

            def first_phase(s, odd, first, last):
                norm = None if last else layer_norm(s + 1)
                dve.wait_ge(q_in_psum, s + 1)
                after(dve, q_sq_ready, s)
                after(dve, q_rows_saved, s)
                after(dve, qT_in_psum, s)
                dve.tensor_tensor(q_tile[:, :, :], PA[:, :].rearrange("p (g e) -> p g e", g=GPS),
                                  bq_b[:, :].unsqueeze(1).to_broadcast([P, GPS, EMB]), ALU.add)\
                    .then_inc(q_tile_ready, 1)
                hidden(s, 0)
                dve.wait_ge(qT_hi_ready, s + 1)
                after(dve, qT_saved, s * (2 * EH * 16))
                dve.tensor_tensor(qT_lo[:, :, :, :].rearrange("p h g r -> p (h g r)"), PB[:, :],
                                  qT_hi[:, :, :, :].rearrange("p h g r -> p (h g r)").bitcast(fp32),
                                  ALU.subtract).then_inc(qT_lo_ready, 1)
                for f in range(FC):
                    if f > 0:
                        hidden(s, f)
                    if f <= 5 and not last:
                        next(norm)
                    if f == 6 and not last:
                        squared_norms(s)
                    if last and f == 2:
                        squared_norms(s)
                        find_shift(0)
                    if last and 4 <= f <= 6:
                        find_shift(f - 3)
                if not last:
                    for _ in norm:
                        raise AssertionError("a seventh part")
                    turn_h(s + 1)
                if not first:
                    add_z(s - 1, PD)
                if not last:
                    split_h(s + 1)

            for _ in layer_norm(0):
                pass
            dve.wait_ge(small_loaded, 48)
            dve.wait_ge(columns_loaded, 64)
            dve.tensor_scalar(b2_b[:, :], b2_b[:, :], 0.5, None, ALU.mult).then_inc(b2_halved, 1)
            turn_h(0)
            dve.wait_ge(w1_low_in_psum, 1)
            dve.tensor_reduce(w1_low_top[:, :], PC[0:1, 0:P], AX.X, ALU.max).then_inc(w1_low_top_ready, 1)
            dve.wait_ge(w1_low_top_ready, 1)
            dve.tensor_scalar(w1_wide[:, :], w1_low_top[:, :], 0.0, None, ALU.is_gt).then_inc(w1_wide_ready, 1)
            split_h(0)
            all_sets(dve, first_phase)

            add_z(SETS - 1, PC)

            def normalise(g, b, n):
                dve.wait_ge(pv_done, n)
                dve.tensor_copy(acc_sb, acc_ps[b]).then_inc(acc_copied, 1)
                dve.wait_ge(acc_turned, n)
                turned = acc_ps[b].rearrange("p (c q m) -> p c q m", q=QS, m=VW)
                dve.reciprocal(rden, turned[:, :, :, HD]).then_inc(rden_ready, 1)
                dve.wait_ge(rden_ready, n)
                dve.tensor_tensor(attn[b].rearrange("p (q c d) -> p c q d", q=QS, d=HD), turned[:, :, :, 0:HD],
                                  rden.unsqueeze(3).to_broadcast([P, CH // QS, QS, HD]), ALU.mult)\
                    .then_inc(attn_ready, 1)

            def project(g, b, n):
                dve.wait_ge(attnT_in_psum, n)
                dve.tensor_copy(attnT.rearrange("p h n -> p (h n)"), acc_ps[b][:, 0:EH * P]).then_inc(attnT_ready, 1)
                dve.wait_ge(s_in_psum, n)
                dve.wait_ge(gated, n)
                dve.tensor_tensor(s_sb[b], acc_ps[b][:, 0:EMB], bu_b[:, :], ALU.add).then_inc(s_ready, 1)

            def attention(g, u, first, last):
                if not first:
                    normalise(g - 1, (u + 1) % 2, g)
                    project(g - 1, (u + 1) % 2, g)

            dve.wait_ge(wu_loaded, 32)
            dve.wait_ge(gate_seeded, SETS)
            all_groups(dve, attention)
            normalise(GROUPS - 1, (GROUPS - 1) % 2, GROUPS)
            project(GROUPS - 1, (GROUPS - 1) % 2, GROUPS)

        @block.tensor
        def _(pe):
            def turn_xn(s):
                pe.wait_ge(xn_ready, s + 1)
                after(pe, q_tile_ready, s)
                for h in range(EH):
                    for g in range(GPS):
                        mm = pe.transpose(PA[:, h * SR + g * P:h * SR + (g + 1) * P],
                                          xn[:, g, h * P:(h + 1) * P], ident[:, :])
                mm.then_inc(xnT_in_psum, 1)

            def turn_hn(s):
                pe.wait_ge(hn_ready, s + 1)
                after(pe, y_sum_ready, s * FC - 1)
                for h in range(EH):
                    for g in range(GPS):
                        mm = pe.transpose(PB[:, h * SR + g * P:h * SR + (g + 1) * P],
                                          hn[:, g, h * P:(h + 1) * P], ident[:, :])
                mm.then_inc(hT_in_psum, 1)

            def project_q(s, groups):
                pe.wait_ge(xnT_ready, s + 1)
                for g in groups:
                    for k in range(EH):
                        mm = pe.matmul(PA[:, g * FB:(g + 1) * FB], xnT[:, k * SR + g * P:k * SR + (g + 1) * P],
                                       wq_sb[:, k, :], start=(k == 0), stop=(k == EH - 1))
                if g == GPS - 1:
                    mm.then_inc(q_in_psum, 1)

            def fc1(s, f, pieces):
                before = max([n for n in range(f) if fc1_ps[n] is fc1_ps[f]], default=-1)
                if before >= 0 or f == 0:
                    after(pe, y_sum_ready, s * FC + before + 1)
                else:
                    pe.wait_ge(qT_lo_ready, s + 1)
                for k in range(EH):
                    for n, (w, h) in enumerate(pieces):
                        mm = pe.matmul(fc1_ps[f][:, k * QT:(k + 1) * QT], w[:, k, f * P:(f + 1) * P],
                                       h[:, k * SR:(k + 1) * SR], start=(n == 0), stop=(n == len(pieces) - 1))
                mm.then_inc(fc1_in_psum, 1)

            def fc2(odd, half, z_ps):
                g = half // 2
                for k in range(half % 2 * FC // 2, (half % 2 + 1) * FC // 2):
                    mm = pe.matmul(z_ps[:, g * FB:(g + 1) * FB], yT[odd][k][:, g * P:(g + 1) * P], w2[:, k, :],
                                   start=(k == 0), stop=(k == FC - 1))
                if half == 2 * GPS - 1:
                    mm.then_inc(fc2_in_psum, 1)

            def first_phase(s, odd, first, last):
                if not first:
                    project_q(s, range(GPS))
                pe.wait_ge(hT_lo_ready, s + 1)
                pe.wait_ge(hT_hi_ready, s + 1)
                with pe.If(w1_wide_reg):
                    ffn(s, odd, first, last, [(w1_lo, hT_lo), (w1_lo, hT_hi), (w1_hi, hT_lo), (w1_hi, hT_hi)])
                with pe.Else():
                    ffn(s, odd, first, last, [(w1_hi, hT_lo), (w1_hi, hT_hi)])

            def ffn(s, odd, first, last, pieces):
                for f in range(FC):
                    if last and 4 <= f <= 6:
                        find_shift(f - 4)
                    fc1(s, f, pieces)
                    if f == 0:
                        pe.wait_ge(q_tile_ready, s + 1)
                        pe.wait_ge(hT_ready, s + 1)
                        for h in range(EH):
                            for g in range(GPS):
                                mm = pe.transpose(PB[:, h * SR + g * P:h * SR + (g + 1) * P],
                                                  q_tile[:, g, h * P:(h + 1) * P], ident[:, :])
                        mm.then_inc(qT_in_psum, 1)
                        after(pe, y_ready, s * FC)
                        if not first:
                            pe.wait_ge(w2_ready, 1)
                    if not last and f == 7:
                        turn_hn(s + 1)
                    if not first:
                        fc2(1 - odd, f, PD)
                    if not last and f == 5:
                        turn_xn(s + 1)

            def find_shift(part):
                if part == 0:
                    pe.wait_ge(shift_step, 1)
                    pe.wait_ge(q_tile_ready, SETS)
                    pe.transpose(PA[0:1, 0:P], norm_max[:, 0:1], ident[:, :]).then_inc(shift_pe, 1)
                elif part == 1:
                    pe.wait_ge(shift_step, 2)
                    pe.matmul(PA[:, QT:QT + 1], ones_row[0:1, :], norm_top[0:1, 0:1], start=True, stop=True)\
                        .then_inc(shift_pe, 1)
                else:
                    pe.wait_ge(scores_wide_ready, 1)
                    wide = pe.value_load(scores_wide[0:1, 0:1])
                    with pe.If(wide):
                        pe.wait_ge(qT_lo_ready, SETS)
                        pe.wait_ge(shift_step, 4)
                        with pe.Fori(0, GROUPS) as g:
                            pe.wait_ge(rowmax_loaded, g * (ROWMAX_DMAS * 16) + ROWMAX_DMAS * 16)
                            for c in range(CH):
                                for h in range(2):
                                    pe.wait_ge(rowmax_reduced, g * (2 * CH) + (2 * c + h + 1))
                                    for j in range(2):
                                        mm = pe.matmul(PA[:, j * QT:(j + 1) * QT], keys[0][:, c * P:(c + 1) * P],
                                                       queries[0][:, (2 * h + j) * QT:(2 * h + j + 1) * QT],
                                                       start=True, stop=True)
                                    mm.then_inc(rowmax_scored, 1)
                    pe.wait_ge(shift_ready, 1)
                    for b in range(4):
                        mm = pe.transpose(PA[:, b * P:(b + 1) * P], shift[:, b * P:(b + 1) * P], ident[:, :])
                    mm.then_inc(shift_pe, 1)

            pe.wait_ge(pool_step, 3)
            turn_xn(0)
            pe.wait_ge(small_loaded, 48)
            project_q(0, range(GPS // 2))
            turn_hn(0)
            project_q(0, range(GPS // 2, GPS))
            pe.wait_ge(w_step, 3)
            pe.transpose(PC[0:1, 0:P], w1_low_sq[:, :], ident[:, :]).then_inc(w1_low_in_psum, 1)
            pe.wait_ge(w1_wide_ready, 1)
            w1_wide_reg = pe.value_load(w1_wide[0:1, 0:1])
            pe.wait_ge(columns_loaded, 64)
            all_sets(pe, first_phase)
            pe.wait_ge(y_sum_ready, SETS * FC)
            pe.wait_ge(y_ready, SETS * FC - FC // 2)
            for half in range(2 * GPS):
                if half == 1:
                    pe.wait_ge(y_ready, SETS * FC)
                fc2(1, half, PC)

            def scores(g, u, c):
                if c == 0:
                    pe.wait_ge(stack_loaded[u % NB], stack_count(g, u % NB))
                for h in range(2):
                    half = (u * CH + c) * 2 + h
                    if h == 1:
                        after(pe, exped, g * (2 * CH) + (2 * c + h - (NB - 1)))
                    for j in range(2):
                        q = 2 * h + j
                        mm = pe.matmul(score_ps[half % NB][:, j * QT:(j + 1) * QT], keys[u % NB][:, c * P:(c + 1) * P],
                                       queries[u % NB][:, q * QT:(q + 1) * QT], start=True, stop=True)
                    mm.then_inc(scored, 1)

            def stack_count(g, b):
                return (g - b) * (STACK_DMAS * 16 // NB) + STACK_DMAS * 16

            def weigh(g, u, c):
                if c == 0:
                    pe.wait_ge(values_ready, g + 1)
                pe.wait_ge(exped, g * (2 * CH) + (2 * c + 2))
                at = ((u * CH + c) % NB) * QS * QT
                for q in range(QS):
                    mm = pe.matmul(acc_ps[u % 2][q * VW:(q + 1) * VW, :], values[u % NB][:, c, :],
                                   ring[:, at + q * QT:at + (q + 1) * QT], start=(c == 0), stop=(c == CH - 1),
                                   skip_group_check=True)
                if c == CH - 1:
                    mm.then_inc(pv_done, 1)

            def turn_acc(b, n):
                pe.wait_ge(acc_copied, n)
                for c in range(QT // P):
                    mm = pe.transpose(acc_ps[b][:, c * P:(c + 1) * P], acc_sb[:, c * P:(c + 1) * P], ident[:, :])
                mm.then_inc(acc_turned, 1)

            def turn_attn(b, n):
                pe.wait_ge(attn_ready, n)
                for h in range(EH):
                    mm = pe.transpose(acc_ps[b][:, h * P:(h + 1) * P], attn[b][:, h * P:(h + 1) * P], ident[:, :])
                mm.then_inc(attnT_in_psum, 1)

            def project(b, n):
                pe.wait_ge(attnT_ready, n)
                for h in range(EH):
                    mm = pe.matmul(acc_ps[b][:, 0:EMB], attnT[:, h, :], wu_sb[:, h, :], start=(h == 0), stop=(h == EH - 1))
                mm.then_inc(s_in_psum, 1)

            def attention(g, u, first, last):
                for c in range(CH):
                    if c + 1 < CH:
                        scores(g, u, c + 1)
                    elif not last:
                        scores(g + 1, (u + 1) % 6, 0)
                    weigh(g, u, c)
                    if not first:
                        b = (u + 1) % 2
                        if c == 1:
                            turn_acc(b, g)
                        if c == 3:
                            turn_attn(b, g)
                        if c == 5:
                            project(b, g)
                        if c == CH - 1:
                            pe.wait_ge(s_ready, g)

            pe.wait_ge(shift_pe, 3)
            pe.wait_ge(y_sum_ready, SETS * FC)
            pe.wait_ge(neg_ready, 2)
            pe.wait_ge(qT_lo_ready, SETS)
            pe.wait_ge(wu_loaded, 32)
            scores(0, 0, 0)
            pe.wait_ge(z_added, SETS)
            all_groups(pe, attention)
            turn_acc((GROUPS - 1) % 2, GROUPS)
            turn_attn((GROUPS - 1) % 2, GROUPS)
            project((GROUPS - 1) % 2, GROUPS)


_INS = ["x", "wqT", "bq", "wuT", "bu", "ln_gamma", "ln_beta", "fc1_q", "fc1_scales", "fc1_bias",
        "fc2_q", "fc2_scales", "fc2_bias"]


def kernel(L0_attn_x, L0_attn_wq, L0_attn_bq, L0_attn_wu, L0_attn_bu, L0_ffn_ln_gamma, L0_ffn_ln_beta,
           L0_ffn_fc1_q, L0_ffn_fc1_scales, L0_ffn_fc1_bias, L0_ffn_fc2_q, L0_ffn_fc2_scales, L0_ffn_fc2_bias):
    import numpy as np
    import concourse.bacc as bacc
    from concourse import mybir as mb
    from concourse.bass_utils import run_bass_kernel_spmd as run

    def columns(a):
        return np.asarray(a).reshape(-1, 128).T

    def by_place(a):
        a = np.asarray(a)
        return a.reshape(a.shape[:-1] + (2, 8, 16)).swapaxes(-1, -2).reshape(a.shape)

    shape = L0_attn_x.shape
    rows = shape[0] * shape[1]
    arrays = [np.asarray(L0_attn_x).reshape(rows, shape[2]), by_place(np.asarray(L0_attn_wq).T), by_place(L0_attn_bq),
              np.asarray(L0_attn_wu).T, L0_attn_bu, columns(L0_ffn_ln_gamma), columns(L0_ffn_ln_beta), L0_ffn_fc1_q,
              np.asarray(L0_ffn_fc1_scales).reshape(2, -1, 128).T, columns(L0_ffn_fc1_bias), L0_ffn_fc2_q, L0_ffn_fc2_scales, L0_ffn_fc2_bias]
    nc = bacc.Bacc("TRN2", target_bir_lowering=False, num_devices=1)
    ins, args = {}, []
    for name, a in zip(_INS, arrays):
        a = np.ascontiguousarray(a)
        ins[f"in_{name}"] = a
        args.append(nc.dram_tensor(f"in_{name}", a.shape, mb.dt.from_np(a.dtype), kind="ExternalInput").ap())
    args.append(nc.dram_tensor("out_rows", (rows, shape[2]), mb.dt.float32, kind="ExternalOutput").ap())
    groups = rows // 128
    args.append(nc.dram_tensor("qT_scratch", (groups, 2, 2, 16, 1024), mb.dt.float32, kind="Internal").ap())
    args.append(nc.dram_tensor("shift_scratch", (2, groups * 16, 128), mb.dt.float32, kind="Internal").ap())
    attention_times_ffn_gate(nc, *args)
    r = run(nc, [ins], core_ids=[0])
    return r.results[0]["out_rows"].reshape(shape)
```
